# Optimizing a Trainium2 kernel written in Bass

```python
import numpy as np
import jax
import jax.numpy as jnp

def _softmax(x, axis=-1):
    return jax.nn.softmax(x, axis=axis)

def _gelu(x):
    return jax.nn.gelu(x, approximate=True)

def _silu(x):
    return jax.nn.silu(x)

def _sigmoid(x):
    return jax.nn.sigmoid(x)

def _layernorm(x, axis=-1, eps=1e-05):
    m = jnp.mean(x, axis=axis, keepdims=True)
    v = jnp.var(x, axis=axis, keepdims=True)
    return (x - m) / jnp.sqrt(v + eps)

def _scatter_add(tgt, idx, src, axis=0):
    return tgt.at[idx].add(src)

def _segment_sum(src, seg, n):
    return jax.ops.segment_sum(src, seg, n)
kernel_name = 'mk_xattn_ffn_d1_seqx_r4_3c2c3c'

def setup_inputs(seed: int=0):
    np.random.seed(seed)
    _w = jnp.asarray

    def _rec_inputs():
        import jax
        import jax.numpy as jnp
        _rk = jax.random.key(seed)
        x = -0.0002928 + 1 * jax.random.normal(jax.random.fold_in(_rk, 1), (16, 256, 256), jnp.float32)
        _lenS = 256 - jax.random.randint(jax.random.fold_in(_rk, 7), (16,), 0, max(1, 256 // 4) + 1, jnp.int32)
        _lenS2 = 256 - jax.random.randint(jax.random.fold_in(_rk, 8), (16,), 0, max(1, 256 // 4) + 1, jnp.int32)
        _ctx_1024P = jax.random.normal(jax.random.fold_in(_rk, 11), (16, 16, 256), jnp.float32)
        _ctx_1024c = jax.random.dirichlet(jax.random.fold_in(_rk, 511), 0.3 * jnp.ones((16,), jnp.float32), (16, 256))
        _ctx_1024t = jnp.einsum('bsk,bkd->bsd', _ctx_1024c, _ctx_1024P)
        _ctx_1024t = _ctx_1024t * jax.lax.rsqrt(jnp.mean(jnp.square(_ctx_1024t)) + 1e-12) * 0.953939
        ctx_1024 = -1.39393e-06 + 0.999914 * (_ctx_1024t + 0.3 * jax.random.normal(jax.random.fold_in(_rk, 611), (16, 256, 256), jnp.float32))
        return (x, ctx_1024)
    x, ctx_1024 = _rec_inputs()

    def _L0_xattn_setup():
        import jax, jax.numpy as jnp
        import numpy as np
        B, S, DIM, NH = (2, 512, 256, 8)
        DH = DIM // NH
        GATE_SOFT_CAP = 15.0
        BACKEND_EPS = 5e-05
        NORM_EPS = 1e-06

        def _mlstm_parallel(q, k, v, i_pre, f_pre):
            log_fg = jax.nn.log_sigmoid(f_pre)
            lf_cs = jnp.cumsum(log_fg, axis=-1)
            lf = jnp.concatenate([jnp.zeros_like(lf_cs[..., :1]), lf_cs], axis=-1)
            log_d = lf[..., 1:, None] - lf[..., None, 1:] + i_pre[..., None, :]
            t_idx = jnp.arange(q.shape[2])
            mask = t_idx[:, None] >= t_idx[None, :]
            log_d = jnp.where(mask, log_d, -jnp.inf)
            m = jnp.max(log_d, axis=-1, keepdims=True)
            d_mat = jnp.exp(log_d - m)
            scores = jnp.einsum('bhtd,bhsd->bhts', q, k) * (1.0 / np.sqrt(DH))
            s_mat = scores * d_mat
            denom = jnp.maximum(jnp.abs(jnp.sum(s_mat, axis=-1, keepdims=True)), jnp.exp(-m)) + BACKEND_EPS
            return jnp.einsum('bhts,bhsd->bhtd', s_mat, v) / denom
        key = jax.random.key(seed)
        kq, kk, kv, kw = jax.random.split(key, 4)
        q = jax.random.normal(kq, (B, S, DIM), dtype=jnp.float32)
        k = jax.random.normal(kk, (B, S, DIM), dtype=jnp.float32)
        v = jax.random.normal(kv, (B, S, DIM), dtype=jnp.float32)
        ifgate_w = 0.02 * jax.random.normal(kw, (2 * NH, 3 * DIM), dtype=jnp.float32)
        ifgate_b = jnp.concatenate([jnp.full((NH,), -10.0, dtype=jnp.float32), jnp.linspace(3.0, 6.0, NH, dtype=jnp.float32)])
        outnorm_w = jnp.zeros((DIM,), dtype=jnp.float32)
        return {'q': q, 'k': k, 'v': v, 'ifgate_w': ifgate_w, 'ifgate_b': ifgate_b, 'outnorm_w': outnorm_w}
    _L0_xattn_all = _L0_xattn_setup()
    _L0_xattn_in = {k: v for k, v in _L0_xattn_all.items() if k in ('ifgate_w', 'ifgate_b', 'outnorm_w')}
    del _L0_xattn_all

    def _L0_ffn_setup():
        import jax, jax.numpy as jnp
        import numpy as np
        D_IN, D_HID = (256, 1024)

        def _ternary(key, shape):
            return jax.random.randint(key, shape, -1, 2).astype(jnp.float32)

        def _tlin(x, w, s):
            return jnp.einsum('bsi,oi->bso', x, w) * s
        key = jax.random.key(seed)
        ks = jax.random.split(key, 12)
        inv = lambda fan: 1.0 / np.sqrt(fan).astype(np.float32)
        return {'x': jax.random.normal(ks[0], (4, 512, D_IN), dtype=jnp.float32), 'w1_w': _ternary(ks[1], (D_HID, D_IN)), 'w1_s': jax.random.uniform(ks[2], (D_HID,), dtype=jnp.float32) * inv(D_IN), 'w2_w': _ternary(ks[3], (D_HID, D_IN)), 'w2_s': jax.random.uniform(ks[4], (D_HID,), dtype=jnp.float32) * inv(D_IN), 'h1_w': _ternary(ks[5], (D_HID, D_HID)), 'h1_s': jax.random.uniform(ks[6], (D_HID,), dtype=jnp.float32) * inv(D_HID), 'h2_w': _ternary(ks[7], (D_HID, D_HID)), 'h2_s': jax.random.uniform(ks[8], (D_HID,), dtype=jnp.float32) * inv(D_HID), 'w3_w': _ternary(ks[9], (D_IN, D_HID)), 'w3_s': jax.random.uniform(ks[10], (D_IN,), dtype=jnp.float32) * inv(D_HID)}
    _L0_ffn_all = _L0_ffn_setup()
    _L0_ffn_in = {k: v for k, v in _L0_ffn_all.items() if k in ('w1_w', 'w1_s', 'w2_w', 'w2_s', 'h1_w', 'h1_s', 'h2_w', 'h2_s', 'w3_w', 'w3_s')}
    del _L0_ffn_all
    return {'x': x, 'ctx_1024': ctx_1024, 'L0_xattn_ifgate_w': _L0_xattn_in['ifgate_w'], 'L0_xattn_ifgate_b': _L0_xattn_in['ifgate_b'], 'L0_xattn_outnorm_w': _L0_xattn_in['outnorm_w'], 'L0_ffn_w1_w': _L0_ffn_in['w1_w'], 'L0_ffn_w1_s': _L0_ffn_in['w1_s'], 'L0_ffn_w2_w': _L0_ffn_in['w2_w'], 'L0_ffn_w2_s': _L0_ffn_in['w2_s'], 'L0_ffn_h1_w': _L0_ffn_in['h1_w'], 'L0_ffn_h1_s': _L0_ffn_in['h1_s'], 'L0_ffn_h2_w': _L0_ffn_in['h2_w'], 'L0_ffn_h2_s': _L0_ffn_in['h2_s'], 'L0_ffn_w3_w': _L0_ffn_in['w3_w'], 'L0_ffn_w3_s': _L0_ffn_in['w3_s']}

def reference(x, ctx_1024, L0_xattn_ifgate_w, L0_xattn_ifgate_b, L0_xattn_outnorm_w, L0_ffn_w1_w, L0_ffn_w1_s, L0_ffn_w2_w, L0_ffn_w2_s, L0_ffn_h1_w, L0_ffn_h1_s, L0_ffn_h2_w, L0_ffn_h2_s, L0_ffn_w3_w, L0_ffn_w3_s):
    import jax
    import jax.numpy as jnp

    def _L0_xattn_ref(q, k, v, ifgate_w, ifgate_b, outnorm_w):
        import jax, jax.numpy as jnp
        import numpy as np
        B, S, DIM, NH = (2, 512, 256, 8)
        DH = DIM // NH
        GATE_SOFT_CAP = 15.0
        BACKEND_EPS = 5e-05
        NORM_EPS = 1e-06

        def _mlstm_parallel(q, k, v, i_pre, f_pre):
            log_fg = jax.nn.log_sigmoid(f_pre)
            lf_cs = jnp.cumsum(log_fg, axis=-1)
            lf = jnp.concatenate([jnp.zeros_like(lf_cs[..., :1]), lf_cs], axis=-1)
            log_d = lf[..., 1:, None] - lf[..., None, 1:] + i_pre[..., None, :]
            t_idx = jnp.arange(q.shape[2])
            mask = t_idx[:, None] >= t_idx[None, :]
            log_d = jnp.where(mask, log_d, -jnp.inf)
            m = jnp.max(log_d, axis=-1, keepdims=True)
            d_mat = jnp.exp(log_d - m)
            scores = jnp.einsum('bhtd,bhsd->bhts', q, k) * (1.0 / np.sqrt(DH))
            s_mat = scores * d_mat
            denom = jnp.maximum(jnp.abs(jnp.sum(s_mat, axis=-1, keepdims=True)), jnp.exp(-m)) + BACKEND_EPS
            return jnp.einsum('bhts,bhsd->bhtd', s_mat, v) / denom
        b, s, dim = q.shape
        gate_in = jnp.concatenate([q, k, v], axis=-1)
        pre = gate_in @ ifgate_w.T + ifgate_b
        pre = GATE_SOFT_CAP * jnp.tanh(pre / GATE_SOFT_CAP)
        i_pre = pre[..., :NH].transpose(0, 2, 1)
        f_pre = pre[..., NH:].transpose(0, 2, 1)
        qh = q.reshape(b, s, NH, DH).transpose(0, 2, 1, 3)
        kh = k.reshape(b, s, NH, DH).transpose(0, 2, 1, 3)
        vh = v.reshape(b, s, NH, DH).transpose(0, 2, 1, 3)
        h = _mlstm_parallel(qh, kh, vh, i_pre, f_pre)
        rrms = jax.lax.rsqrt(jnp.mean(h * h, axis=-1, keepdims=True) + NORM_EPS)
        gain = (1.0 + outnorm_w).reshape(1, NH, 1, DH)
        h = h * rrms * gain
        return h.transpose(0, 2, 1, 3).reshape(b, s, dim)

    def _L0_ffn_ref(x, w1_w, w1_s, w2_w, w2_s, h1_w, h1_s, h2_w, h2_s, w3_w, w3_s):
        import jax, jax.numpy as jnp
        import numpy as np
        D_IN, D_HID = (256, 1024)

        def _ternary(key, shape):
            return jax.random.randint(key, shape, -1, 2).astype(jnp.float32)

        def _tlin(x, w, s):
            return jnp.einsum('bsi,oi->bso', x, w) * s
        h = jax.nn.silu(_tlin(x, w1_w, w1_s)) * _tlin(x, w2_w, w2_s)
        h = jax.nn.gelu(_tlin(h, h1_w, h1_s), approximate=False)
        h = jax.nn.gelu(_tlin(h, h2_w, h2_s), approximate=False)
        return _tlin(h, w3_w, w3_s)
    x = x + _L0_xattn_ref(_layernorm(x, axis=-1), ctx_1024, ctx_1024, L0_xattn_ifgate_w, L0_xattn_ifgate_b, L0_xattn_outnorm_w)
    x = x + _L0_ffn_ref(_layernorm(x, axis=-1), L0_ffn_w1_w, L0_ffn_w1_s, L0_ffn_w2_w, L0_ffn_w2_s, L0_ffn_h1_w, L0_ffn_h1_s, L0_ffn_h2_w, L0_ffn_h2_s, L0_ffn_w3_w, L0_ffn_w3_s)
    return x

_drawn_inputs = setup_inputs


def setup_inputs(seed=0):
    import zlib

    import numpy as np

    out = dict(_drawn_inputs(seed))
    spreads = {'L0_xattn_outnorm_w': (0.0, 0.1)}
    factors = {}
    for name, (base, spread) in spreads.items():
        noise = np.random.default_rng([zlib.crc32(name.encode()), seed]).standard_normal(out[name].shape)
        drawn = base * np.exp(spread * noise) if base else spread * noise
        out[name] = jnp.asarray(drawn.astype(out[name].dtype))
    for name, factor in factors.items():
        out[name] = (out[name] * factor).astype(out[name].dtype)
    return out
```

```python
from contextlib import ExitStack

import numpy as np

import concourse.bass as bass
from concourse import mybir

ALU = mybir.AluOpType
ACT = mybir.ActivationFunctionType
AX = mybir.AxisListType
F32 = mybir.dt.float32
F32R = mybir.dt.float32r
BF16 = mybir.dt.bfloat16
I32 = mybir.dt.int32

P = 128
BATCH, SEQ, DIM = 16, 256, 256
HEADS, DH = 8, 32
HID = 1024
TILES = SEQ // P
CH = DIM // P
KH = HID // P
ROWGRP = P // DH
DV = DH + 1
CAP = 15.0
SCORE_SCALE = float(1.0 / np.sqrt(DH))
BACKEND_EPS, RMS_EPS, LN_EPS = 5e-05, 1e-06, 1e-05
MASKED = 1e30
RSQRT_SEED = 0x5F3759DF

UNIT = 1024
N_W1 = CH * HID // UNIT
UNIT_W1, UNIT_W2 = 0, N_W1
UNIT_H1 = 2 * N_W1
UNIT_H2 = UNIT_H1 + KH
UNIT_W3 = UNIT_H2 + KH
UNITS = UNIT_W3 + KH * DIM // UNIT
STAGE = 4

ROW_G, ROW_FLOOR, ROW_CHUNK = 0, 32, 64
ROWS = ROW_CHUNK + HEADS
GATE_COLS = ROW_FLOOR + HEADS

RSQRT_STEPS = 11
NORM_STEPS = TILES + 2 + RSQRT_STEPS
MIX_STEPS = 7 + RSQRT_STEPS
SCAN_STEPS = 6
RESIDUAL_STEPS = 3

LEAD = 2


def build(nc, x, ctx_tok, ctx_t, gate_w, gate_b, outnorm_w, w_all, scales, w3_s, out):
    with ExitStack() as stack:
        def sb(name, shape, dt=F32):
            return stack.enter_context(nc.sbuf_tensor(name, shape, dt))

        def sem(name):
            return stack.enter_context(nc.semaphore(name))

        m_rows = nc.dram_tensor("m_rows", [HEADS, SEQ], F32, kind="Internal").ap()

        wgt = sb("wgt", [P, UNITS * UNIT], F32R)
        stage = sb("stage", [P, STAGE, UNIT])
        h_hi = [sb(f"h_hi{n}", [P, KH, SEQ], F32R) for n in range(2)]
        h_lo = [sb(f"h_lo{n}", [P, KH, SEQ], F32R) for n in range(2)]
        z2_hi = sb("z2_hi", [P, CH, SEQ], F32R)
        z2_lo = sb("z2_lo", [P, CH, SEQ], F32R)
        silu_a = sb("silu_a", [P, 2, SEQ])
        h_f = sb("h_f", [P, 2, SEQ])
        gelu_f = sb("gelu_f", [P, 2, SEQ])
        scl = sb("scl", [P, 4, KH])
        w3s_b = sb("w3s_b", [P, DIM])
        gain_b = sb("gain_b", [P, DIM])
        ident = sb("ident", [P, P])
        head_mask = sb("head_mask", [P, CH, ROWGRP, DV])
        gw_in = sb("gw_in", [P, 3 * CH, 2 * HEADS])
        gw = sb("gw", [P, 2 * CH, GATE_COLS])
        gb_in = sb("gb_in", [GATE_COLS, 1])
        gb = sb("gb", [GATE_COLS, 1])

        x_in = sb("x_in", [P, TILES, DIM])
        x1 = sb("x1", [P, TILES, DIM])
        x1_ffn = sb("x1_ffn", [P, TILES, DIM])
        x_res = sb("x_res", [P, TILES, DIM])
        y_scaled = sb("y_scaled", [P, TILES, DIM])
        y_out = sb("y_out", [P, TILES, DIM])
        ctxT = sb("ctxT", [P, CH, SEQ])
        v_aug = sb("v_aug", [P, TILES, HEADS, DV])
        k_wt = sb("k_wt", [P, HEADS, DH])
        z = sb("z", [P, TILES, DIM])
        z2 = sb("z2", [P, TILES, DIM])
        zT = sb("zT", [P, CH, SEQ])
        rows = sb("rows", [ROWS, SEQ])
        f_row = sb("f_row", [HEADS, SEQ])
        m_row = sb("m_row", [HEADS, SEQ])
        m_all = sb("m_all", [P, HEADS, SEQ])
        cols = sb("cols", [P, TILES, ROWS])
        e_cols = sb("e_cols", [P, TILES, 2, HEADS])
        floor = sb("floor", [P, TILES, HEADS])
        smat = sb("smat", [P, ROWGRP, TILES, CH, P])
        state = sb("state", [P, CH * ROWGRP * DV])
        num = sb("num", [P, TILES, HEADS, DV])
        far = sb("far", [P, HEADS, DV])
        h_att = sb("h_att", [P, TILES * HEADS, DH])
        h_sq = sb("h_sq", [P, TILES * HEADS, DH])
        stats = sb("stats", [P, TILES, 6])
        mv = sb("mv", [P, TILES, 2])
        nw = sb("nw", [P, 4, TILES * HEADS])
        rms = sb("rms", [P, 4, TILES * HEADS])
        inexact = sb("inexact", [P, UNITS])
        inexact_sum = sb("inexact_sum", [P, 1])
        general = sb("general", [1, 1], I32)
        ones = sb("ones", [P, 1])
        den = sb("den", [P, 2, TILES * HEADS])

        ps_f = [stack.enter_context(nc.psum_tensor(f"ps_f{n}", [P, 2, SEQ], F32)) for n in range(4)]
        ps_a = [stack.enter_context(nc.psum_tensor(f"ps_a{n}", [P, 512], F32)) for n in range(4)]

        s_alone = sem("s_alone")
        s_gb0 = sem("s_gb0")
        s_cleared = sem("s_cleared")
        s_const = sem("s_const")
        s_ready = sem("s_ready")
        s_ident = sem("s_ident")
        s_unit = [sem(f"s_unit{n}") for n in range(STAGE)]
        s_wgt = sem("s_wgt")
        s_inexact = sem("s_inexact")
        s_inexact_sum = sem("s_inexact_sum")
        s_inexact_all = sem("s_inexact_all")
        s_general = sem("s_general")
        s_xin = sem("s_xin")
        s_ctxT = sem("s_ctxT")
        s_v = sem("s_v")
        s_norm1 = sem("s_norm1")
        s_z = sem("s_z")
        s_xres = sem("s_xres")
        s_zT = sem("s_zT")
        s_zTe = sem("s_zTe")
        s_gate = sem("s_gate")
        s_gact = sem("s_gact")
        s_scan = sem("s_scan")
        s_mst = sem("s_mst")
        s_mall = sem("s_mall")
        s_mask = sem("s_mask")
        s_colT = sem("s_colT")
        s_cols = sem("s_cols")
        s_ecols = sem("s_ecols")
        s_floor = sem("s_floor")
        s_exp = sem("s_exp")
        s_qk = sem("s_qk")
        s_smat = sem("s_smat")
        s_kwt = sem("s_kwt")
        s_st = sem("s_st")
        s_state = sem("s_state")
        s_pv = sem("s_pv")
        s_farmm = sem("s_farmm")
        s_far = sem("s_far")
        s_near = sem("s_near")
        s_num = sem("s_num")
        s_mix = sem("s_mix")
        s_resid = sem("s_resid")
        s_norm2 = sem("s_norm2")
        s_z2 = sem("s_z2")
        s_z2T = sem("s_z2T")
        s_z2hi = sem("s_z2hi")
        s_z2lo = sem("s_z2lo")
        s_x1f = sem("s_x1f")
        s_ab = sem("s_ab")
        s_silu = sem("s_silu")
        s_hf = sem("s_hf")
        s_hi1 = sem("s_hi1")
        s_lo1 = sem("s_lo1")
        s_mm = sem("s_mm")
        s_gelu = sem("s_gelu")
        s_hi = sem("s_hi")
        s_lo = sem("s_lo")
        s_ymm = sem("s_ymm")
        s_ysc = sem("s_ysc")
        s_y = sem("s_y")
        s_out = sem("s_out")

        def x1_ready(j):
            return RESIDUAL_STEPS * (j + 1)

        def reuse(eng, semaphore, value):
            if not (isinstance(value, int) and value == 0):
                eng.wait_ge(semaphore, value)

        ORDER = [u for n in range(N_W1) for u in (UNIT_W1 + n, UNIT_W2 + n)] + list(range(UNIT_H1, UNITS))
        PER_SLOT = [len(range(n, UNITS, STAGE)) for n in range(STAGE)]

        def unit_landed(i, u):
            q = ORDER.index(u)
            return s_unit[q % STAGE], 16 * (PER_SLOT[q % STAGE] * (i + 1) + q // STAGE + 1)

        block = stack.enter_context(nc.Block())

        def load_x(eng, j):
            reuse(eng, s_xres, j)
            eng.sem_inc(s_alone, 1)
            eng.dma_start(x_in[:], x[bass.ds(j, 1)].rearrange("b p t d -> (b p) t d")).then_inc(s_xin, 16)

        def load_context(eng, j):
            reuse(eng, s_qk, j)
            eng.sem_inc(s_alone, 1)
            eng.dma_start(ctxT[:], ctx_t[bass.ds(j, 1)].rearrange("b p c t -> (b p) c t")).then_inc(s_ctxT, 16)
            reuse(eng, s_pv, j)
            eng.sem_inc(s_alone, 1)
            eng.dma_start(v_aug[:], ctx_tok[bass.ds(j, 1)].rearrange("b p t h d -> (b p) t h d")).then_inc(s_v, 16)

        def spread_max(eng, j):
            eng.wait_ge(s_scan, SCAN_STEPS * j + 3)
            eng.sem_inc(s_alone, 1)
            eng.dma_start(m_rows, m_row[:]).then_inc(s_mst, 16)
            eng.wait_ge(s_mst, 16 * j + 16)
            eng.sem_inc(s_alone, 1)
            eng.dma_start(m_all[:], m_rows.rearrange("(o h) t -> o h t", o=1).to_broadcast([P, HEADS, SEQ])).then_inc(s_mall, 16)

        @block.sync
        def _(sp):
            load_x(sp, 0)
            load_context(sp, 0)
            sp.dma_start(gw_in[:], gate_w).then_inc(s_const, 16)
            sp.wait_ge(s_gb0, 1)
            sp.dma_start(gb_in[ROW_G:ROW_G + HEADS], gate_b[0]).then_inc(s_const, 16)
            sp.dma_start(gb_in[ROW_FLOOR:ROW_FLOOR + HEADS], gate_b[1]).then_inc(s_const, 16)
            sp.dma_start(gain_b[:], outnorm_w.to_broadcast([P, DIM])).then_inc(s_const, 16)
            sp.dma_start(scl[:], scales).then_inc(s_const, 16)
            sp.dma_start(w3s_b[:], w3_s.to_broadcast([P, DIM])).then_inc(s_const, 16)
            def load_units(units):
                for u in units:
                    if u >= STAGE:
                        sp.wait_ge(s_inexact, u - STAGE + 1)
                    sp.dma_start(stage[:, u % STAGE], w_all[u]).then_inc(s_unit[u % STAGE], 16)

            load_units(range(0, 4))
            load_x(sp, 1)
            spread_max(sp, 0)
            load_units(range(4, 16))
            load_context(sp, 1)
            load_x(sp, 2)
            load_units(range(16, 20))
            spread_max(sp, 1)
            load_units(range(20, UNITS))
            load_context(sp, 2)

            def stream(i, part):
                for q in part:
                    if STAGE <= q < 2 * STAGE:
                        sp.wait_ge(s_ab, KH * i + (KH // 2 if q < STAGE + 2 else KH))
                    elif q >= 2 * STAGE:
                        sp.wait_ge(s_mm, 2 * KH * i + q - 2 * STAGE + 1)
                    sp.sem_inc(s_alone, 1)
                    sp.dma_start(stage[:, q % STAGE], w_all[ORDER[q]]).then_inc(s_unit[q % STAGE], 16)

            def streamed(i):
                sp.wait_ge(s_ymm, TILES * i + TILES)
                sp.sem_inc(s_alone, 1)

            def attention_loads(j):
                spread_max(sp, j)
                load_x(sp, j + 1)
                load_context(sp, j + 1)

            sp.wait_ge(s_general, 1)
            flag = sp.value_load(general[0:1, 0:1])
            with sp.If(flag == 0):
                with sp.Fori(LEAD, BATCH - 1) as j:
                    attention_loads(j)
                spread_max(sp, BATCH - 1)
            with sp.Else():
                with sp.Fori(LEAD, BATCH - 1) as j:
                    stream(j - LEAD, range(0, 6))
                    spread_max(sp, j)
                    stream(j - LEAD, range(6, 13))
                    load_x(sp, j + 1)
                    stream(j - LEAD, range(13, UNITS))
                    load_context(sp, j + 1)
                    streamed(j - LEAD)
                for i in range(BATCH - 1 - LEAD, BATCH):
                    stream(i, range(0, 6))
                    if i + LEAD < BATCH:
                        spread_max(sp, i + LEAD)
                    stream(i, range(6, UNITS))
                    streamed(i)

        @block.gpsimd
        def _(pool):
            pool.memset(gb_in[:], 0.0).then_inc(s_gb0, 1)
            pool.memset(ident[:], 0.0).then_inc(s_ident, 1)
            pool.memset(head_mask[:], SCORE_SCALE).then_inc(s_ident, 1)
            pool.wait_ge(s_ident, 2)
            pool.affine_select(out=ident[:], in_=ident[:], compare_op=ALU.not_equal, fill=1.0, base=0,
                               pattern=[[-1, P]], channel_multiplier=1).then_inc(s_ident, 1)
            pool.affine_select(out=head_mask[:], in_=head_mask[:], compare_op=ALU.is_ge, fill=0.0, base=0,
                               pattern=[[0, CH], [-DH, ROWGRP], [0, DV]], channel_multiplier=1).then_inc(s_ident, 1)
            pool.wait_ge(s_ident, 4)
            pool.affine_select(out=head_mask[:], in_=head_mask[:], compare_op=ALU.is_ge, fill=0.0, base=DH - 1,
                               pattern=[[0, CH], [DH, ROWGRP], [0, DV]], channel_multiplier=-1).then_inc(s_ident, 1)

            def mask_future(j):
                pool.wait_ge(s_mall, 16 * j + 16)
                pool.sem_inc(s_alone, 1)
                for t in range(TILES):
                    part = m_all[:, :, t * P:(t + 1) * P]
                    pool.affine_select(out=part, in_=part, compare_op=ALU.is_ge, fill=MASKED, base=0,
                                       pattern=[[0, HEADS], [1, P]], channel_multiplier=-1).then_inc(s_mask, 1)

            def weigh_keys(j):
                pool.wait_ge(s_ecols, j + 1)
                pool.wait_ge(s_v, 16 * j + 16)
                reuse(pool, s_st, j)
                w = e_cols[:, 0, 1, :].rearrange("p (h o) -> p h o", o=1).to_broadcast([P, HEADS, DH])
                pool.tensor_tensor(k_wt[:], v_aug[:, 0, :, 0:DH], w, ALU.mult).then_inc(s_kwt, 1)

            def keep_tokens(j):
                pool.wait_ge(s_z, j + 1)
                reuse(pool, s_resid, x1_ready(j - 1) if not isinstance(j, int) or j else 0)
                pool.sem_inc(s_alone, 1)
                pool.tensor_copy(x_res[:], x_in[:]).then_inc(s_xres, 1)

            def residual(j):
                pool.wait_ge(s_mix, MIX_STEPS * (j + 1))
                rr = rms[:, 3].rearrange("p (h o) -> p h o", o=1).to_broadcast([P, TILES * HEADS, DH])
                pool.tensor_tensor(h_att[:], h_att[:], rr, ALU.mult).then_inc(s_resid, 1)
                pool.wait_ge(s_resid, RESIDUAL_STEPS * j + 1)
                for t in range(TILES):
                    h = h_att[:, t * HEADS:(t + 1) * HEADS].rearrange("p h d -> p (h d)")
                    last = pool.tensor_tensor(h, h, gain_b[:], ALU.mult)
                last.then_inc(s_resid, 1)
                pool.wait_ge(s_resid, RESIDUAL_STEPS * j + 2)
                reuse(pool, s_x1f, j)
                pool.tensor_tensor(x1[:].rearrange("p t d -> p (t d)"), h_att[:].rearrange("p h d -> p (h d)"),
                                   x_res[:].rearrange("p t d -> p (t d)"), ALU.add).then_inc(s_resid, 1)

            def keep_residual(i):
                pool.wait_ge(s_resid, x1_ready(i))
                pool.sem_inc(s_alone, 1)
                pool.tensor_copy(x1_ffn[:], x1[:]).then_inc(s_x1f, 1)

            def store(i):
                pool.wait_ge(s_y, TILES * i + TILES)
                pool.sem_inc(s_alone, 1)
                pool.dma_start(out[bass.ds(i, 1)].rearrange("b p t d -> (b p) t d"), y_out[:]).then_inc(s_out, 16)
                pool.wait_ge(s_out, 16 * i + 16)
                pool.sem_inc(s_alone, 1)

            def batch(i, ahead, start):
                keep_residual(i)
                if ahead:
                    residual(i + 1)
                if start:
                    keep_tokens(i + LEAD)
                    mask_future(i + LEAD)
                    weigh_keys(i + LEAD)
                store(i)

            pool.memset(ones[:], 1.0).then_inc(s_ident, 1)
            keep_tokens(0)
            mask_future(0)
            weigh_keys(0)
            residual(0)
            keep_tokens(1)
            mask_future(1)
            weigh_keys(1)
            with pool.Fori(0, BATCH - LEAD) as i:
                batch(i, True, True)
            batch(BATCH - 2, True, False)
            batch(BATCH - 1, False, False)
            pool.wait_ge(s_mst, 16 * BATCH)

        @block.scalar
        def _(act):
            def take_zT(j):
                act.wait_ge(s_zT, j + 1)
                act.activation(zT[:].rearrange("p c t -> p (c t)"), ps_a[0][:], ACT.Copy).then_inc(s_zTe, 1)

            def soft_cap(j):
                act.wait_ge(s_gate, j + 1)
                act.activation(rows[ROW_G:ROW_G + HEADS], ps_a[1][ROW_G:ROW_G + HEADS, 0:SEQ], ACT.Tanh,
                               bias=gb[ROW_G:ROW_G + HEADS], scale=1.0 / CAP).then_inc(s_gact, 1)
                act.activation(f_row[:], ps_a[1][ROW_FLOOR:ROW_FLOOR + HEADS, 0:SEQ], ACT.Tanh,
                               bias=gb[ROW_FLOOR:ROW_FLOOR + HEADS], scale=1.0 / CAP).then_inc(s_gact, 1)

            def softplus(j):
                act.wait_ge(s_gact, 4 * j + 2)
                act.activation(f_row[:], f_row[:], ACT.Exp, scale=-CAP).then_inc(s_gact, 1)
                act.wait_ge(s_gact, 4 * j + 3)
                act.activation(f_row[:], f_row[:], ACT.Ln, bias=1.0).then_inc(s_gact, 1)

            def decay(j):
                act.wait_ge(s_cols, j + 1)
                for k, r0 in enumerate((ROW_FLOOR, ROW_CHUNK)):
                    last = act.activation(e_cols[:, :, k, :], cols[:, :, r0:r0 + HEADS], ACT.Exp)
                last.then_inc(s_ecols, 1)
                act.wait_ge(s_mask, TILES * (j + 1))
                reuse(act, s_pv, j)
                for r in range(ROWGRP):
                    for t in range(TILES):
                        for c in range(CH):
                            h = c * ROWGRP + r
                            last = act.activation(smat[:, r, t, c, :], m_all[:, h, t * P:(t + 1) * P], ACT.Exp,
                                                  bias=cols[:, t, ROW_G + h:ROW_G + h + 1], scale=-1.0)
                    last.then_inc(s_exp, 1)

            def take_near(j):
                act.wait_ge(s_pv, j + 1)
                act.activation(num[:, 0].rearrange("p h d -> p (h d)"), ps_a[0][:, 0:HEADS * DV], ACT.Copy).then_inc(s_near, 1)

            def take_z2T(j):
                act.wait_ge(s_z2T, j + 1)
                act.activation(z2_hi[:].rearrange("p c t -> p (c t)"), ps_a[0][:], ACT.Copy).then_inc(s_z2hi, 1)

            def silu(i, m):
                act.wait_ge(s_ab, KH * i + m + 1)
                act.activation(silu_a[:, m % 2], ps_f[m % 4][:, 0], ACT.Silu, scale=scl[:, 0, m:m + 1]).then_inc(s_silu, 1)

            def hi_1(i, m):
                act.wait_ge(s_hf, KH * i + m + 1)
                act.activation(h_hi[0][:, m], h_f[:, m % 2], ACT.Copy).then_inc(s_hi1, 1)

            def gelu(i, layer, m):
                n = 2 * KH * i + KH * layer + m
                act.wait_ge(s_mm, n + 1)
                if not (layer == 0 and m < 2):
                    act.wait_ge(s_lo, n - 1)
                act.activation(gelu_f[:, m % 2], ps_f[m % 4][:, 0], ACT.Gelu,
                               scale=scl[:, 2 + layer, m:m + 1]).then_inc(s_gelu, 1)
                act.wait_ge(s_gelu, n + 1)
                act.activation(h_hi[1 - layer][:, m], gelu_f[:, m % 2], ACT.Copy).then_inc(s_hi, 1)

            def convert(units):
                for u in units:
                    act.wait_ge(s_unit[u % STAGE], 16 * (u // STAGE + 1))
                    act.activation(wgt[:, u * UNIT:(u + 1) * UNIT], stage[:, u % STAGE], ACT.Copy).then_inc(s_wgt, 1)

            def batch(i, ahead, start):
                j = i + LEAD
                for m in range(KH):
                    silu(i, m)
                    if m >= 1:
                        hi_1(i, m - 1)
                    if start and m == 4:
                        take_zT(j)
                hi_1(i, KH - 1)
                if start:
                    soft_cap(j)
                    softplus(j)
                for m in range(KH):
                    gelu(i, 0, m)
                if start:
                    decay(j)
                for m in range(KH):
                    if ahead and m == 1:
                        take_z2T(i + 1)
                    gelu(i, 1, m)
                if start:
                    take_near(j)

            act.wait_ge(s_ready, 1)
            convert(range(0, 2))
            take_zT(0)
            soft_cap(0)
            softplus(0)
            convert(range(2, 12))
            decay(0)
            convert(range(12, 16))
            take_near(0)
            take_zT(1)
            soft_cap(1)
            softplus(1)
            convert(range(16, UNITS))
            take_z2T(0)
            decay(1)
            take_near(1)
            with act.Fori(0, BATCH - LEAD) as i:
                batch(i, True, True)
            batch(BATCH - 2, True, False)
            batch(BATCH - 1, False, False)

        @block.vector
        def _(dve):
            count = {}

            def link(chain, base, ins):
                count[chain] = count.get(chain, 0) + 1
                ins.then_inc(chain, 1)
                dve.wait_ge(chain, base + count[chain])

            def rsqrt(chain, base, work, n):
                v, half, prod, y = (work[:, k, 0:n] for k in range(4))
                link(chain, base, dve.tensor_scalar(half.bitcast(I32), v.bitcast(I32), 1, None, ALU.logical_shift_right))
                link(chain, base, dve.tensor_scalar(y.bitcast(I32), half.bitcast(I32), -1.0, float(RSQRT_SEED), ALU.mult, ALU.add))
                for _ in range(3):
                    link(chain, base, dve.tensor_tensor(prod, y, y, ALU.mult))
                    link(chain, base, dve.scalar_tensor_tensor(prod, prod, -0.5, v, ALU.mult, ALU.mult))
                    link(chain, base, dve.scalar_tensor_tensor(y, prod, 1.5, y, ALU.add, ALU.mult))

            def layernorm(chain, j, src, dst, done):
                base = NORM_STEPS * j
                count[chain] = 0
                for t in range(TILES):
                    link(chain, base, dve.bn_stats(stats[:, t], src[:, t]))
                dve.sem_inc(s_alone, 1)
                for t in range(TILES):
                    last = dve.bn_aggr(mv[:, t], stats[:, t])
                link(chain, base, last)
                link(chain, base, dve.tensor_scalar(nw[:, 0, 0:TILES], mv[:, :, 1], LN_EPS, None, ALU.add))
                rsqrt(chain, base, nw, TILES)
                for t in range(TILES):
                    last = dve.tensor_scalar(dst[:, t], src[:, t], mv[:, t, 0:1], nw[:, 3, t:t + 1], ALU.subtract, ALU.mult)
                last.then_inc(done, 1)
                dve.wait_ge(done, j + 1)
                assert count[chain] == NORM_STEPS

            def norm_1(j):
                dve.wait_ge(s_xin, 16 * j + 16)
                reuse(dve, s_zT, j)
                layernorm(s_norm1, j, x_in, z, s_z)

            def norm_2(j):
                dve.wait_ge(s_resid, x1_ready(j))
                reuse(dve, s_z2T, j)
                layernorm(s_norm2, j, x1, z2, s_z2)

            def scans(j):
                dve.wait_ge(s_gact, 4 * j + 4)
                n = SCAN_STEPS * j
                dve.tensor_tensor_scan(f_row[:], f_row[:], f_row[:], 0.0, ALU.add, ALU.max).then_inc(s_scan, 1)
                dve.wait_ge(s_scan, n + 1)
                g = rows[ROW_G:ROW_G + HEADS]
                dve.scalar_tensor_tensor(g, g, CAP, f_row[:], ALU.mult, ALU.add).then_inc(s_scan, 1)
                dve.wait_ge(s_scan, n + 2)
                reuse(dve, s_mst, 16 * j)
                dve.tensor_tensor_scan(m_row[:], g, g, -MASKED, ALU.max, ALU.max).then_inc(s_scan, 1)
                dve.wait_ge(s_scan, n + 3)
                c = m_row[:, P - 1:P]
                dve.tensor_tensor(rows[ROW_FLOOR:ROW_FLOOR + HEADS], f_row[:], m_row[:], ALU.subtract).then_inc(s_scan, 1)
                dve.tensor_scalar(rows[ROW_CHUNK:ROW_CHUNK + HEADS, 0:P], g[:, 0:P], c, None, ALU.subtract).then_inc(s_scan, 1)
                dve.tensor_scalar(rows[ROW_CHUNK:ROW_CHUNK + HEADS, P:SEQ], m_row[:, P:SEQ], -1.0, c, ALU.mult, ALU.add)\
                   .then_inc(s_scan, 1)

            def take_cols(j):
                dve.wait_ge(s_colT, j + 1)
                dve.tensor_copy(cols[:].rearrange("p t r -> p (t r)"), ps_a[1][:, 0:TILES * ROWS]).then_inc(s_cols, 1)

            def weigh_scores(j, groups):
                if 0 in groups:
                    dve.wait_ge(s_ecols, j + 1)
                    dve.tensor_scalar(floor[:], e_cols[:, :, 0, :], BACKEND_EPS, None, ALU.add).then_inc(s_floor, 1)
                    dve.wait_ge(s_qk, j + 1)
                for r in groups:
                    dve.wait_ge(s_exp, ROWGRP * j + r + 1)
                    s = smat[:, r].rearrange("p t c q -> p (t c q)")
                    dve.scalar_tensor_tensor(s, ps_a[r][:], SCORE_SCALE, s, ALU.mult, ALU.mult).then_inc(s_smat, 1)

            def take_state(j):
                dve.wait_ge(s_st, j + 1)
                dve.tensor_tensor(state[:], ps_a[2][:, 0:CH * ROWGRP * DV],
                                  head_mask[:].rearrange("p c h d -> p (c h d)"), ALU.mult).then_inc(s_state, 1)

            def take_far(j):
                dve.wait_ge(s_farmm, j + 1)
                u = e_cols[:, 1, 1, :].rearrange("p (h o) -> p h o", o=1).to_broadcast([P, HEADS, DV])
                dve.tensor_tensor(far[:], ps_a[3][:, 0:HEADS * DV].rearrange("p (h d) -> p h d", d=DV), u, ALU.mult)\
                   .then_inc(s_far, 1)
                dve.wait_ge(s_far, j + 1)
                dve.tensor_tensor(num[:, 1], ps_a[1][:, 0:HEADS * DV].rearrange("p (h d) -> p h d", d=DV), far[:], ALU.add)\
                   .then_inc(s_num, 1)

            def mix(j):
                count[s_mix] = 0
                base = MIX_STEPS * j
                n = num[:].rearrange("p t h d -> p (t h) d")
                total = n[:, :, DH]
                dve.wait_ge(s_near, j + 1)
                dve.wait_ge(s_num, j + 1)
                dve.wait_ge(s_floor, j + 1)
                link(s_mix, base, dve.scalar_tensor_tensor(den[:, 0], total, -1.0, total, ALU.mult, ALU.max))
                link(s_mix, base, dve.scalar_tensor_tensor(den[:, 0], den[:, 0], BACKEND_EPS,
                                                           floor[:].rearrange("p t h -> p (t h)"), ALU.add, ALU.max))
                link(s_mix, base, dve.reciprocal(den[:, 1], den[:, 0]))
                per_head = den[:, 1].rearrange("p (h o) -> p h o", o=1).to_broadcast([P, TILES * HEADS, DH])
                link(s_mix, base, dve.tensor_tensor(h_att[:], n[:, :, 0:DH], per_head, ALU.mult))
                link(s_mix, base, dve.tensor_tensor(h_sq[:], h_att[:], h_att[:], ALU.mult))
                link(s_mix, base, dve.tensor_reduce(rms[:, 2], h_sq[:], AX.X, ALU.add))
                link(s_mix, base, dve.tensor_scalar(rms[:, 0], rms[:, 2], 1.0 / DH, RMS_EPS, ALU.mult, ALU.add))
                rsqrt(s_mix, base, rms, TILES * HEADS)
                assert count[s_mix] == MIX_STEPS

            def take_z2T(j):
                dve.wait_ge(s_z2hi, j + 1)
                dve.tensor_tensor(z2_lo[:].rearrange("p c t -> p (c t)"), ps_a[0][:],
                                  z2_hi[:].rearrange("p c t -> p (c t)").bitcast(F32), ALU.subtract).then_inc(s_z2lo, 1)

            def swiglu(i, m):
                n = KH * i + m
                dve.wait_ge(s_silu, n + 1)
                if m >= 2:
                    dve.wait_ge(s_lo1, n - 1)
                dve.scalar_tensor_tensor(h_f[:, m % 2], ps_f[m % 4][:, 1], scl[:, 1, m:m + 1], silu_a[:, m % 2],
                                         ALU.mult, ALU.mult).then_inc(s_hf, 1)

            def lo_1(i, m):
                dve.wait_ge(s_hi1, KH * i + m + 1)
                dve.tensor_tensor(h_lo[0][:, m], h_f[:, m % 2], h_hi[0][:, m].bitcast(F32), ALU.subtract).then_inc(s_lo1, 1)

            def lo(i, layer, m):
                dve.wait_ge(s_hi, 2 * KH * i + KH * layer + m + 1)
                dve.tensor_tensor(h_lo[1 - layer][:, m], gelu_f[:, m % 2], h_hi[1 - layer][:, m].bitcast(F32),
                                  ALU.subtract).then_inc(s_lo, 1)

            def finish(i):
                for t in range(TILES):
                    dve.wait_ge(s_ymm, TILES * i + t + 1)
                    dve.tensor_tensor(y_scaled[:, t], ps_f[t][:, 0], w3s_b[:], ALU.mult).then_inc(s_ysc, 1)
                dve.wait_ge(s_x1f, i + 1)
                for t in range(TILES):
                    dve.wait_ge(s_ysc, TILES * (i + 1) + t + 1)
                    dve.tensor_tensor(y_out[:, t], y_scaled[:, t], x1_ffn[:, t], ALU.add).then_inc(s_y, 1)

            def collect(units):
                for u in units:
                    dve.wait_ge(s_wgt, u + 1)
                    if u >= 2:
                        dve.wait_ge(s_inexact, u - 1)
                    marks = (silu_a, gelu_f)[u % 2][:].rearrange("p n t -> p (n t)").bitcast(BF16)
                    dve.scalar_tensor_tensor(marks, stage[:, u % STAGE], 1.0, wgt[:, u * UNIT:(u + 1) * UNIT].bitcast(F32),
                                             ALU.mult, ALU.not_equal, accum_out=inexact[:, u:u + 1]).then_inc(s_inexact, 1)

            def decide():
                dve.wait_ge(s_inexact, UNITS)
                dve.tensor_reduce(inexact_sum[:], inexact[:], AX.X, ALU.add).then_inc(s_inexact_sum, 1)
                dve.wait_ge(s_inexact_all, 1)
                dve.tensor_scalar(general[:], ps_f[3][0:1, 0, 0:1], 0.0, None, ALU.is_gt).then_inc(s_general, 1)

            def batch(i, ahead, start, more):
                j = i + LEAD
                for m in range(KH):
                    swiglu(i, m)
                    if m >= 1:
                        lo_1(i, m - 1)
                lo_1(i, KH - 1)
                for m in range(KH):
                    lo(i, 0, m)
                    if start and m == 0:
                        scans(j)
                    if ahead and m == 1:
                        mix(i + 1)
                    if ahead and m == 6:
                        norm_2(i + 1)
                    if start and m == 5:
                        take_cols(j)
                for m in range(KH):
                    lo(i, 1, m)
                    if ahead and m == 0:
                        take_z2T(i + 1)
                    if start and m in (2, 3):
                        weigh_scores(j, range(2 * (m - 2), 2 * (m - 1)))
                    if start and m == 4:
                        take_state(j)
                    if more and m == 5:
                        norm_1(j + 1)
                    if start and m == 7:
                        take_far(j)
                finish(i)

            dve.sem_inc(s_ysc, TILES)
            dve.memset(rows[:], 0.0).then_inc(s_cleared, 1)
            dve.memset(gw[:], 0.0).then_inc(s_cleared, 1)
            dve.wait_ge(s_cleared, 2)
            dve.wait_ge(s_ident, 6)
            norm_1(0)
            dve.wait_ge(s_const, 16 * 6)
            for k, r0 in enumerate((ROW_G, ROW_FLOOR)):
                w = gw_in[:, :, k * HEADS:(k + 1) * HEADS]
                dve.tensor_copy(gw[:, 0:CH, r0:r0 + HEADS], w[:, 0:CH])
                dve.tensor_tensor(gw[:, CH:2 * CH, r0:r0 + HEADS], w[:, CH:2 * CH], w[:, 2 * CH:3 * CH], ALU.add)
            dve.tensor_scalar(gb[:], gb_in[:], 1.0 / CAP, None, ALU.mult)
            dve.tensor_scalar(gain_b[:], gain_b[:], 1.0, None, ALU.add).then_inc(s_ready, 1)
            dve.wait_ge(s_ready, 1)
            collect(range(0, 4))
            scans(0)
            take_cols(0)
            norm_1(1)
            collect(range(4, 12))
            weigh_scores(0, range(ROWGRP))
            take_state(0)
            take_far(0)
            mix(0)
            collect(range(12, 18))
            scans(1)
            take_cols(1)
            norm_2(0)
            collect(range(18, UNITS))
            decide()
            take_z2T(0)
            norm_1(2)
            weigh_scores(1, range(ROWGRP))
            take_state(1)
            take_far(1)
            with dve.Fori(0, BATCH - LEAD - 1) as i:
                batch(i, True, True, True)
            batch(BATCH - LEAD - 1, True, True, False)
            batch(BATCH - 2, True, False, False)
            batch(BATCH - 1, False, False, False)

        @block.tensor
        def _(pe):
            def turn(src, done):
                for c in range(CH):
                    for t in range(TILES):
                        col = c * SEQ + t * P
                        last = pe.transpose(ps_a[0][:, col:col + P], src[:, t, c * P:(c + 1) * P], ident[:])
                last.then_inc(done, 1)

            def turn_z(j):
                pe.wait_ge(s_z, j + 1)
                reuse(pe, s_near, j)
                turn(z, s_zT)

            def turn_z2(j):
                pe.wait_ge(s_z2, j + 1)
                turn(z2, s_z2T)

            def gates(j):
                pe.wait_ge(s_zTe, j + 1)
                pe.wait_ge(s_ctxT, 16 * j + 16)
                reuse(pe, s_num, j)
                for c in range(CH):
                    pe.matmul(ps_a[1][0:GATE_COLS, 0:SEQ], gw[:, CH + c], ctxT[:, c], start=(c == 0), stop=False)
                for c in range(CH):
                    last = pe.matmul(ps_a[1][0:GATE_COLS, 0:SEQ], gw[:, c], zT[:, c], start=False, stop=(c == CH - 1))
                last.then_inc(s_gate, 1)

            def turn_rows(j):
                pe.wait_ge(s_scan, SCAN_STEPS * j + SCAN_STEPS)
                for t in range(TILES):
                    last = pe.transpose(ps_a[1][:, t * ROWS:(t + 1) * ROWS], rows[:, t * P:(t + 1) * P], ident[0:ROWS, 0:ROWS])
                last.then_inc(s_colT, 1)

            def scores(j):
                pe.wait_ge(s_cols, j + 1)
                reuse(pe, s_z2lo, j)
                for t in range(TILES):
                    for c in range(CH):
                        for r in range(ROWGRP):
                            d = slice(r * DH, (r + 1) * DH)
                            col = (t * CH + c) * P
                            last = pe.matmul(ps_a[r][:, col:col + P], ctxT[d, c, t * P:(t + 1) * P],
                                             zT[d, c, t * P:(t + 1) * P], start=True, stop=True)
                last.then_inc(s_qk, 1)

            def make_state(j):
                pe.wait_ge(s_kwt, j + 1)
                pe.wait_ge(s_smat, ROWGRP * j + 3)
                for c in range(CH):
                    h = slice(c * ROWGRP, (c + 1) * ROWGRP)
                    last = pe.matmul(ps_a[2][:, c * ROWGRP * DV:(c + 1) * ROWGRP * DV], k_wt[:, h, :], v_aug[:, 0, h, :],
                                     start=True, stop=True)
                last.then_inc(s_st, 1)

            def values(j):
                pe.wait_ge(s_smat, ROWGRP * j + ROWGRP)
                pe.wait_ge(s_v, 16 * j + 16)
                for t in range(TILES):
                    for h in range(HEADS):
                        last = pe.matmul(ps_a[t][:, h * DV:(h + 1) * DV], smat[:, h % ROWGRP, t, h // ROWGRP, :],
                                         v_aug[:, t, h, :], start=True, stop=True)
                last.then_inc(s_pv, 1)

            def read_state(j):
                pe.wait_ge(s_state, j + 1)
                for c in range(CH):
                    part = slice(c * ROWGRP * DV, (c + 1) * ROWGRP * DV)
                    last = pe.matmul(ps_a[3][:, part], zT[:, c, P:SEQ], state[:, part], start=True, stop=True)
                last.then_inc(s_farmm, 1)

            def columns(u, col, width, as_is):
                if as_is:
                    return stage[:, ORDER.index(u) % STAGE, col:col + width]
                return wgt[:, u * UNIT + col:u * UNIT + col + width]

            def moving(a, as_is):
                return a.bitcast(F32) if as_is else a

            def swiglu(i, m, as_is):
                if m < TILES:
                    pe.wait_ge(s_ysc, TILES * i + m + 1)
                if m >= 4:
                    pe.wait_ge(s_hf, KH * i + m - 3)
                per = KH // N_W1
                for half, base in enumerate((UNIT_W1, UNIT_W2)):
                    if as_is and m % per == 0:
                        pe.wait_ge(*unit_landed(i, base + m // per))
                    for c in range(CH):
                        w = columns(base + m // per, (m % per * CH + c) * P, P, as_is)
                        pe.matmul(ps_f[m % 4][:, half], w, moving(z2_hi[:, c], as_is), start=(c == 0), stop=False)
                        last = pe.matmul(ps_f[m % 4][:, half], w, moving(z2_lo[:, c], as_is), start=False, stop=(c == CH - 1))
                last.then_inc(s_ab, 1)

            def hidden(i, layer, m, ks, as_is):
                group = KH * layer + m
                unit = UNIT_H1 + group
                if ks[0] == 0:
                    if as_is:
                        pe.wait_ge(*unit_landed(i, unit))
                    if group >= 4:
                        pe.wait_ge(s_gelu, 2 * KH * i + group - 3)
                for k in ks:
                    if layer == 0:
                        if m < 2:
                            pe.wait_ge(s_lo1, KH * i + max(k + 1, m + 5))
                        elif m < 4 and k == 0:
                            pe.wait_ge(s_lo1, KH * i + KH)
                    elif m < 2:
                        pe.wait_ge(s_lo, 2 * KH * i + k + 1)
                    w = columns(unit, k * P, P, as_is)
                    pe.matmul(ps_f[m % 4][:, 0], w, moving(h_hi[layer][:, k], as_is), start=(k == 0), stop=False)
                    last = pe.matmul(ps_f[m % 4][:, 0], w, moving(h_lo[layer][:, k], as_is), start=False, stop=(k == KH - 1))
                if ks[-1] == KH - 1:
                    last.then_inc(s_mm, 1)

            def hidden_layer(i, layer, as_is, after):
                for m in range(2):
                    hidden(i, layer, m, range(KH - 1), as_is)
                for m in range(2):
                    hidden(i, layer, m, range(KH - 1, KH), as_is)
                    after(m)
                for m in range(2, KH):
                    hidden(i, layer, m, range(KH), as_is)
                    after(m)

            def project(i, as_is):
                per = UNIT // DIM

                def part(t, ks):
                    for k in ks:
                        if as_is and k % per == 0:
                            pe.wait_ge(*unit_landed(i, UNIT_W3 + k // per))
                        pe.wait_ge(s_lo, 2 * KH * i + KH + max(k + 1, t + 5))
                        w = columns(UNIT_W3 + k // per, k % per * DIM, DIM, as_is)
                        pe.matmul(ps_f[t][:, 0], moving(h_hi[0][:, k, t * P:(t + 1) * P], as_is), w, start=(k == 0), stop=False)
                        last = pe.matmul(ps_f[t][:, 0], moving(h_lo[0][:, k, t * P:(t + 1) * P], as_is), w, start=False,
                                         stop=(k == KH - 1))
                    return last

                for t in range(TILES):
                    part(t, range(KH - 1))
                for t in range(TILES):
                    part(t, range(KH - 1, KH)).then_inc(s_ymm, 1)

            def batch(i, ahead, start, as_is):
                j = i + LEAD
                pe.wait_ge(s_z2lo, i + 1)
                for m in range(KH):
                    swiglu(i, m, as_is)
                    if start and m == 2:
                        turn_z(j)
                if start:
                    gates(j)

                def after_2(m):
                    if start and m == 5:
                        turn_rows(j)

                def after_3(m):
                    if ahead and m == 0:
                        turn_z2(i + 1)
                    if start and m == 3:
                        scores(j)
                    if start and m == 5:
                        make_state(j)
                    if start and m == 7:
                        values(j)
                        read_state(j)

                hidden_layer(i, 0, as_is, after_2)
                hidden_layer(i, 1, as_is, after_3)
                project(i, as_is)

            def batches(as_is):
                with pe.Fori(0, BATCH - LEAD) as i:
                    batch(i, True, True, as_is)
                batch(BATCH - 2, True, False, as_is)
                batch(BATCH - 1, False, False, as_is)

            def attend(j):
                scores(j)
                make_state(j)
                values(j)
                read_state(j)

            pe.wait_ge(s_ident, 6)
            pe.wait_ge(s_cleared, 2)
            turn_z(0)
            pe.wait_ge(s_ready, 1)
            gates(0)
            turn_rows(0)
            attend(0)
            turn_z(1)
            gates(1)
            turn_rows(1)
            turn_z2(0)
            pe.wait_ge(s_inexact_sum, 1)
            pe.matmul(ps_f[3][0:1, 0, 0:1], inexact_sum[:], ones[:], start=True, stop=True).then_inc(s_inexact_all, 1)
            attend(1)
            pe.wait_ge(s_wgt, UNITS)
            pe.wait_ge(s_general, 1)
            flag = pe.value_load(general[0:1, 0:1])
            with pe.If(flag == 0):
                batches(False)
            with pe.Else():
                batches(True)


def kernel(x, ctx_1024, L0_xattn_ifgate_w, L0_xattn_ifgate_b, L0_xattn_outnorm_w, L0_ffn_w1_w, L0_ffn_w1_s, L0_ffn_w2_w,
           L0_ffn_w2_s, L0_ffn_h1_w, L0_ffn_h1_s, L0_ffn_h2_w, L0_ffn_h2_s, L0_ffn_w3_w, L0_ffn_w3_s):
    import concourse.bacc as bacc
    from concourse.bass_utils import run_bass_kernel_spmd

    def tok(a):
        return np.ascontiguousarray(np.asarray(a).reshape(BATCH, TILES, P, DIM).transpose(0, 2, 1, 3))

    ctx = np.asarray(ctx_1024)
    v_aug = np.ones((BATCH, P, TILES, HEADS, DV), np.float32)
    v_aug[..., 0:DH] = tok(ctx).reshape(BATCH, P, TILES, HEADS, DH)
    ctx_t = np.ascontiguousarray(ctx.reshape(BATCH, SEQ, CH, P).transpose(0, 3, 2, 1))

    def up(w):
        return np.asarray(w).reshape(N_W1, KH // N_W1, P, CH, P).transpose(0, 4, 1, 3, 2).reshape(N_W1, P, UNIT)

    def square(w):
        return np.asarray(w).reshape(KH, P, KH, P).transpose(0, 3, 2, 1).reshape(KH, P, UNIT)

    def down(w):
        n = KH * DIM // UNIT
        return np.asarray(w).reshape(DIM, n, KH // n, P).transpose(1, 3, 2, 0).reshape(n, P, UNIT)

    w_all = np.ascontiguousarray(np.concatenate([up(L0_ffn_w1_w), up(L0_ffn_w2_w), square(L0_ffn_h1_w), square(L0_ffn_h2_w),
                                                 down(L0_ffn_w3_w)]))
    scales = np.ascontiguousarray(np.stack([np.asarray(s).reshape(KH, P) for s in
                                            (L0_ffn_w1_s, L0_ffn_w2_s, L0_ffn_h1_s, L0_ffn_h2_s)]).transpose(2, 0, 1))
    gate_w = np.ascontiguousarray(np.asarray(L0_xattn_ifgate_w).reshape(2 * HEADS, 3 * CH, P).transpose(2, 1, 0))
    arrays = {
        "x": tok(x), "ctx_tok": v_aug, "ctx_t": ctx_t, "gate_w": gate_w,
        "gate_b": np.ascontiguousarray(np.asarray(L0_xattn_ifgate_b).reshape(2, HEADS, 1)),
        "outnorm_w": np.ascontiguousarray(np.asarray(L0_xattn_outnorm_w).reshape(1, DIM)),
        "w_all": w_all, "scales": scales, "w3_s": np.ascontiguousarray(np.asarray(L0_ffn_w3_s).reshape(1, DIM)),
    }
    nc = bacc.Bacc("TRN2", target_bir_lowering=False, num_devices=1)
    args = {n: nc.dram_tensor(n, a.shape, F32, kind="ExternalInput").ap() for n, a in arrays.items()}
    out = nc.dram_tensor("out", (BATCH, P, TILES, DIM), F32, kind="ExternalOutput").ap()
    build(nc, out=out, **args)
    got = run_bass_kernel_spmd(nc, [arrays], core_ids=[0]).results[0]["out"]
    return np.ascontiguousarray(np.asarray(got).transpose(0, 2, 1, 3).reshape(BATCH, SEQ, DIM))
```

```python
from contextlib import ExitStack

import numpy as np

import concourse.bass as bass
from concourse import mybir

ALU = mybir.AluOpType
ACT = mybir.ActivationFunctionType
AX = mybir.AxisListType
F32 = mybir.dt.float32
F32R = mybir.dt.float32r
BF16 = mybir.dt.bfloat16
I32 = mybir.dt.int32

P = 128
BATCH, SEQ, DIM = 16, 256, 256
HEADS, DH = 8, 32
HID = 1024
TILES = SEQ // P
CH = DIM // P
KH = HID // P
ROWGRP = P // DH
DV = DH + 1
CAP = 15.0
SCORE_SCALE = float(1.0 / np.sqrt(DH))
BACKEND_EPS, RMS_EPS, LN_EPS = 5e-05, 1e-06, 1e-05
MASKED = 1e30
RSQRT_SEED = 0x5F3759DF

UNIT = 1024
N_W1 = CH * HID // UNIT
UNIT_W1, UNIT_W2 = 0, N_W1
UNIT_H1 = 2 * N_W1
UNIT_H2 = UNIT_H1 + KH
UNIT_W3 = UNIT_H2 + KH
UNITS = UNIT_W3 + KH * DIM // UNIT
COLS = UNITS * UNIT
PER_LOAD = 2
GELU = 4
STAGE = 4
COMPARE = COLS // BATCH

ROW_G, ROW_FLOOR, ROW_CHUNK = 0, 32, 64
ROWS = ROW_CHUNK + HEADS
GATE_COLS = ROW_FLOOR + HEADS

RSQRT_STEPS = 11
NORM_STEPS = TILES + 2 + RSQRT_STEPS
MIX_STEPS = 7 + RSQRT_STEPS
SCAN_STEPS = 6
RESIDUAL_STEPS = 3

LAST_BANKS = (2, 3)

LEAD = 2


def build(nc, x, ctx_tok, ctx_t, gate_w, gate_b, outnorm_w, w_cols, scales, w3_s, out):
    with ExitStack() as stack:
        def sb(name, shape, dt=F32):
            return stack.enter_context(nc.sbuf_tensor(name, shape, dt))

        def sem(name):
            return stack.enter_context(nc.semaphore(name))

        x1_kept = nc.dram_tensor("x1_kept", [BATCH, P, TILES, DIM], F32, kind="Internal").ap()
        m_rows = nc.dram_tensor("m_rows", [HEADS, SEQ], F32, kind="Internal").ap()

        wgt = sb("wgt", [P, COLS], F32R)
        stage = sb("stage", [P, STAGE * UNIT])
        raw = stage[:, 0:COMPARE]
        marks = stage[:, COMPARE:COMPARE + COMPARE // 2].bitcast(BF16)
        h_hi = [sb(f"h_hi{n}", [P, KH, SEQ], F32R) for n in range(2)]
        h_lo = [sb(f"h_lo{n}", [P, KH, SEQ], F32R) for n in range(2)]
        z2_hi = sb("z2_hi", [P, CH, SEQ], F32R)
        z2_lo = sb("z2_lo", [P, CH, SEQ], F32R)
        silu_a = sb("silu_a", [P, 2, SEQ])
        h_f = sb("h_f", [P, 2, SEQ])
        gelu_f = sb("gelu_f", [P, GELU, SEQ])
        scl = sb("scl", [P, 4, KH])
        w3s_b = sb("w3s_b", [P, DIM])
        gain_b = sb("gain_b", [P, DIM])
        ident = sb("ident", [P, P])
        head_mask = sb("head_mask", [P, CH, ROWGRP, DV])
        gw_in = sb("gw_in", [P, 3 * CH, 2 * HEADS])
        gw = sb("gw", [P, 2 * CH, GATE_COLS])
        gb_in = sb("gb_in", [GATE_COLS, 1])
        gb = sb("gb", [GATE_COLS, 1])

        x_in = sb("x_in", [P, TILES, DIM])
        x1 = sb("x1", [P, TILES, DIM])
        x1_ffn = sb("x1_ffn", [P, TILES, DIM])
        x_res = sb("x_res", [P, TILES, DIM])
        y_out = sb("y_out", [P, TILES, DIM])
        ctxT = sb("ctxT", [P, CH, SEQ])
        v_aug = sb("v_aug", [P, TILES, HEADS, DV])
        k_wt = sb("k_wt", [P, HEADS, DH])
        z = sb("z", [P, TILES, DIM])
        z2 = sb("z2", [P, TILES, DIM])
        zT = sb("zT", [P, CH, SEQ])
        rows = sb("rows", [ROWS, SEQ])
        f_row = sb("f_row", [HEADS, SEQ])
        m_row = sb("m_row", [HEADS, SEQ])
        m_all = sb("m_all", [P, HEADS, SEQ])
        cols = sb("cols", [P, TILES, ROWS])
        e_cols = sb("e_cols", [P, TILES, 2, HEADS])
        floor = sb("floor", [P, TILES, HEADS])
        smat = sb("smat", [P, ROWGRP, TILES, CH, P])
        state = sb("state", [P, CH * ROWGRP * DV])
        num = sb("num", [P, TILES, HEADS, DV])
        far = sb("far", [P, HEADS, DV])
        h_att = sb("h_att", [P, TILES * HEADS, DH])
        h_sq = sb("h_sq", [P, TILES * HEADS, DH])
        stats = sb("stats", [P, TILES, 6])
        mv = sb("mv", [P, TILES, 2])
        nw = sb("nw", [P, 4, TILES * HEADS])
        rms = sb("rms", [P, 4, TILES * HEADS])
        inexact = sb("inexact", [P, BATCH])
        inexact_sum = sb("inexact_sum", [P, 1])
        general = sb("general", [1, 1], I32)
        ones = sb("ones", [P, 1])
        den = sb("den", [P, 2, TILES * HEADS])

        ps_f = [stack.enter_context(nc.psum_tensor(f"ps_f{n}", [P, 2, SEQ], F32)) for n in range(4)]
        ps_a = [stack.enter_context(nc.psum_tensor(f"ps_a{n}", [P, 512], F32)) for n in range(4)]

        s_alone = sem("s_alone")
        s_gb0 = sem("s_gb0")
        s_cleared = sem("s_cleared")
        s_const = sem("s_const")
        s_ready = sem("s_ready")
        s_ident = sem("s_ident")
        s_wgt = sem("s_wgt")
        s_raw = sem("s_raw")
        s_inexact = sem("s_inexact")
        s_inexact_sum = sem("s_inexact_sum")
        s_inexact_all = sem("s_inexact_all")
        s_general = sem("s_general")
        s_unit = [sem(f"s_unit{n}") for n in range(STAGE)]
        s_x1in = sem("s_x1in")
        s_xin = sem("s_xin")
        s_ctxT = sem("s_ctxT")
        s_v = sem("s_v")
        s_norm1 = sem("s_norm1")
        s_z = sem("s_z")
        s_xres = sem("s_xres")
        s_zT = sem("s_zT")
        s_zTe = sem("s_zTe")
        s_gate = sem("s_gate")
        s_gact = sem("s_gact")
        s_scan = sem("s_scan")
        s_mst = sem("s_mst")
        s_mall = sem("s_mall")
        s_decay = sem("s_decay")
        s_mask = sem("s_mask")
        s_colT = sem("s_colT")
        s_cols = sem("s_cols")
        s_ecols = sem("s_ecols")
        s_floor = sem("s_floor")
        s_exp = sem("s_exp")
        s_qk = sem("s_qk")
        s_smat = sem("s_smat")
        s_kwt = sem("s_kwt")
        s_st = sem("s_st")
        s_state = sem("s_state")
        s_pv = sem("s_pv")
        s_farmm = sem("s_farmm")
        s_far = sem("s_far")
        s_near = sem("s_near")
        s_num = sem("s_num")
        s_mix = sem("s_mix")
        s_resid = sem("s_resid")
        s_x1kept = sem("s_x1kept")
        s_norm2 = sem("s_norm2")
        s_z2 = sem("s_z2")
        s_z2T = sem("s_z2T")
        s_z2hi = sem("s_z2hi")
        s_z2lo = sem("s_z2lo")
        s_x1f = sem("s_x1f")
        s_ab = sem("s_ab")
        s_silu = sem("s_silu")
        s_hf = sem("s_hf")
        s_hi1 = sem("s_hi1")
        s_lo1 = sem("s_lo1")
        s_mm = sem("s_mm")
        s_gelu = sem("s_gelu")
        s_hi = sem("s_hi")
        s_lo = sem("s_lo")
        s_ymm = sem("s_ymm")
        s_ysc = sem("s_ysc")
        s_y = sem("s_y")
        s_out = sem("s_out")

        def x1_ready(j):
            return RESIDUAL_STEPS * (j + 1)

        def reuse(eng, semaphore, value):
            if not (isinstance(value, int) and value == 0):
                eng.wait_ge(semaphore, value)

        ORDER = [u for n in range(N_W1) for u in (UNIT_W1 + n, UNIT_W2 + n)] + list(range(UNIT_H1, UNITS))
        PER_SLOT = [len(range(n, UNITS, STAGE)) for n in range(STAGE)]

        def unit_landed(i, u):
            q = ORDER.index(u)
            return s_unit[q % STAGE], 16 * (PER_SLOT[q % STAGE] * i + q // STAGE + 1)

        def if_general(eng, path):
            eng.wait_ge(s_general, 1)
            with eng.If(eng.value_load(general[0:1, 0:1]) != 0):
                with eng.Fori(0, BATCH) as i:
                    path(i)

        block = stack.enter_context(nc.Block())

        def load_x(eng, j):
            reuse(eng, s_xres, j)
            eng.sem_inc(s_alone, 1)
            eng.dma_start(x_in[:], x[bass.ds(j, 1)].rearrange("b p t d -> (b p) t d")).then_inc(s_xin, 16)

        def load_context(eng, j):
            reuse(eng, s_qk, j)
            eng.sem_inc(s_alone, 1)
            eng.dma_start(ctxT[:], ctx_t[bass.ds(j, 1)].rearrange("b p c t -> (b p) c t")).then_inc(s_ctxT, 16)
            reuse(eng, s_pv, j)
            eng.sem_inc(s_alone, 1)
            eng.dma_start(v_aug[:], ctx_tok[bass.ds(j, 1)].rearrange("b p t h d -> (b p) t h d")).then_inc(s_v, 16)

        def spread_max(eng, j):
            eng.wait_ge(s_scan, SCAN_STEPS * j + 3)
            eng.sem_inc(s_alone, 1)
            reuse(eng, s_exp, ROWGRP * j)
            eng.sem_inc(s_alone, 1)
            eng.dma_start(m_rows, m_row[:]).then_inc(s_mst, 16)
            eng.wait_ge(s_mst, 16 * j + 16)
            eng.sem_inc(s_alone, 1)
            eng.dma_start(m_all[:], m_rows.rearrange("(o h) t -> o h t", o=1).to_broadcast([P, HEADS, SEQ])).then_inc(s_mall, 16)

        def keep_x1(eng, j):
            eng.wait_ge(s_resid, x1_ready(j))
            eng.sem_inc(s_alone, 1)
            eng.dma_start(x1_kept[bass.ds(j, 1)].rearrange("b p t d -> (b p) t d"), x1[:]).then_inc(s_x1kept, 16)

        def load_raw(eng, i):
            reuse(eng, s_inexact, i)
            eng.sem_inc(s_alone, 1)
            eng.dma_start(raw, w_cols[:, bass.ds(i * COMPARE, COMPARE)]).then_inc(s_raw, 16)

        @block.sync
        def _(sp):
            load_x(sp, 0)
            load_context(sp, 0)
            sp.dma_start(gw_in[:], gate_w).then_inc(s_const, 16)
            sp.wait_ge(s_gb0, 1)
            sp.dma_start(gb_in[ROW_G:ROW_G + HEADS], gate_b[0]).then_inc(s_const, 16)
            sp.dma_start(gb_in[ROW_FLOOR:ROW_FLOOR + HEADS], gate_b[1]).then_inc(s_const, 16)
            sp.dma_start(gain_b[:], outnorm_w.to_broadcast([P, DIM])).then_inc(s_const, 16)
            sp.dma_start(scl[:], scales).then_inc(s_const, 16)
            sp.dma_start(w3s_b[:], w3_s.to_broadcast([P, DIM])).then_inc(s_const, 16)
            load_x(sp, 1)
            spread_max(sp, 0)
            load_context(sp, 1)
            load_raw(sp, 0)
            keep_x1(sp, 0)
            load_x(sp, 2)
            spread_max(sp, 1)
            load_context(sp, 2)
            with sp.Fori(0, BATCH - LEAD - 1) as i:
                spread_max(sp, i + LEAD)
                keep_x1(sp, i + 1)
                load_x(sp, i + LEAD + 1)
                load_raw(sp, i + 1)
                load_context(sp, i + LEAD + 1)
            spread_max(sp, BATCH - 1)
            for i in range(BATCH - LEAD - 1, BATCH - 1):
                keep_x1(sp, i + 1)
                load_raw(sp, i + 1)
            sp.wait_ge(s_mst, 16 * BATCH)
            sp.wait_ge(s_x1kept, 16 * BATCH)

            def general_path(i):
                g = BATCH + i
                sp.wait_ge(s_x1f, g)
                sp.sem_inc(s_alone, 1)
                sp.wait_ge(s_z2, g)
                sp.sem_inc(s_alone, 1)
                sp.dma_start(x1[:], x1_kept[bass.ds(i, 1)].rearrange("b p t d -> (b p) t d")).then_inc(s_x1in, 16)
                for q, u in enumerate(ORDER):
                    if q < STAGE:
                        sp.wait_ge(s_ymm, TILES * g)
                    elif q < 2 * STAGE:
                        sp.wait_ge(s_ab, KH * g + (KH // 2 if q < STAGE + 2 else KH))
                    else:
                        sp.wait_ge(s_mm, 2 * KH * g + q - 2 * STAGE + 1)
                    sp.sem_inc(s_alone, 1)
                    sp.dma_start(stage[:, q % STAGE * UNIT:(q % STAGE + 1) * UNIT], w_cols[:, u * UNIT:(u + 1) * UNIT])\
                      .then_inc(s_unit[q % STAGE], 16)

            if_general(sp, general_path)

        @block.gpsimd
        def _(pool):
            pool.memset(gb_in[:], 0.0).then_inc(s_gb0, 1)
            pool.memset(ident[:], 0.0).then_inc(s_ident, 1)
            pool.memset(head_mask[:], SCORE_SCALE).then_inc(s_ident, 1)
            pool.wait_ge(s_ident, 2)
            pool.affine_select(out=ident[:], in_=ident[:], compare_op=ALU.not_equal, fill=1.0, base=0,
                               pattern=[[-1, P]], channel_multiplier=1).then_inc(s_ident, 1)
            pool.affine_select(out=head_mask[:], in_=head_mask[:], compare_op=ALU.is_ge, fill=0.0, base=0,
                               pattern=[[0, CH], [-DH, ROWGRP], [0, DV]], channel_multiplier=1).then_inc(s_ident, 1)
            pool.wait_ge(s_ident, 4)
            pool.affine_select(out=head_mask[:], in_=head_mask[:], compare_op=ALU.is_ge, fill=0.0, base=DH - 1,
                               pattern=[[0, CH], [DH, ROWGRP], [0, DV]], channel_multiplier=-1).then_inc(s_ident, 1)

            def decay_exponents(j):
                pool.wait_ge(s_mall, 16 * j + 16)
                pool.sem_inc(s_alone, 1)
                pool.wait_ge(s_cols, j + 1)
                pool.sem_inc(s_alone, 1)
                for t in range(TILES):
                    part = m_all[:, :, t * P:(t + 1) * P]
                    g = cols[:, t, ROW_G:ROW_G + HEADS].rearrange("p (h o) -> p h o", o=1).to_broadcast([P, HEADS, P])
                    pool.tensor_tensor(part, part, g, ALU.subtract).then_inc(s_decay, 1)
                    pool.wait_ge(s_decay, TILES * j + t + 1)
                    pool.sem_inc(s_alone, 1)
                    pool.affine_select(out=part, in_=part, compare_op=ALU.is_ge, fill=MASKED, base=0,
                                       pattern=[[0, HEADS], [1, P]], channel_multiplier=-1).then_inc(s_mask, 1)

            def weigh_keys(j):
                pool.wait_ge(s_ecols, j + 1)
                pool.wait_ge(s_v, 16 * j + 16)
                reuse(pool, s_st, j)
                w = e_cols[:, 0, 1, :].rearrange("p (h o) -> p h o", o=1).to_broadcast([P, HEADS, DH])
                pool.tensor_tensor(k_wt[:], v_aug[:, 0, :, 0:DH], w, ALU.mult).then_inc(s_kwt, 1)

            def keep_tokens(j):
                pool.wait_ge(s_z, j + 1)
                reuse(pool, s_resid, x1_ready(j - 1) if not isinstance(j, int) or j else 0)
                pool.sem_inc(s_alone, 1)
                pool.tensor_copy(x_res[:], x_in[:]).then_inc(s_xres, 1)

            def residual(j):
                pool.wait_ge(s_mix, MIX_STEPS * (j + 1))
                rr = rms[:, 3].rearrange("p (h o) -> p h o", o=1).to_broadcast([P, TILES * HEADS, DH])
                pool.tensor_tensor(h_att[:], h_att[:], rr, ALU.mult).then_inc(s_resid, 1)
                pool.wait_ge(s_resid, RESIDUAL_STEPS * j + 1)
                for t in range(TILES):
                    h = h_att[:, t * HEADS:(t + 1) * HEADS].rearrange("p h d -> p (h d)")
                    last = pool.tensor_tensor(h, h, gain_b[:], ALU.mult)
                last.then_inc(s_resid, 1)
                pool.wait_ge(s_resid, RESIDUAL_STEPS * j + 2)
                reuse(pool, s_x1f, j)
                pool.sem_inc(s_alone, 1)
                reuse(pool, s_x1kept, 16 * j)
                pool.sem_inc(s_alone, 1)
                pool.tensor_tensor(x1[:].rearrange("p t d -> p (t d)"), h_att[:].rearrange("p h d -> p (h d)"),
                                   x_res[:].rearrange("p t d -> p (t d)"), ALU.add).then_inc(s_resid, 1)

            def keep_residual(i):
                pool.sem_inc(s_alone, 1)
                pool.tensor_copy(x1_ffn[:], x1[:]).then_inc(s_x1f, 1)

            def store(i, b):
                pool.wait_ge(s_y, TILES * i + TILES)
                pool.sem_inc(s_alone, 1)
                pool.dma_start(out[bass.ds(b, 1)].rearrange("b p t d -> (b p) t d"), y_out[:]).then_inc(s_out, 16)
                pool.wait_ge(s_out, 16 * i + 16)
                pool.sem_inc(s_alone, 1)

            def batch(i, ahead, start):
                pool.wait_ge(s_resid, x1_ready(i))
                keep_residual(i)
                if ahead:
                    residual(i + 1)
                if start:
                    keep_tokens(i + LEAD)
                    decay_exponents(i + LEAD)
                    weigh_keys(i + LEAD)
                store(i, i)

            pool.memset(ones[:], 1.0).then_inc(s_ident, 1)
            for u in range(0, UNITS, PER_LOAD):
                part = slice(u * UNIT, (u + PER_LOAD) * UNIT)
                pool.dma_start(wgt[:, part], w_cols[:, part]).then_inc(s_wgt, 16)
            keep_tokens(0)
            decay_exponents(0)
            weigh_keys(0)
            residual(0)
            keep_tokens(1)
            decay_exponents(1)
            weigh_keys(1)
            with pool.Fori(0, BATCH - LEAD) as i:
                batch(i, True, True)
            batch(BATCH - 2, True, False)
            batch(BATCH - 1, False, False)

            def general_path(i):
                pool.wait_ge(s_x1in, 16 * i + 16)
                keep_residual(BATCH + i)
                store(BATCH + i, i)

            if_general(pool, general_path)

        @block.scalar
        def _(act):
            def take_zT(j):
                act.wait_ge(s_zT, j + 1)
                act.activation(zT[:].rearrange("p c t -> p (c t)"), ps_a[0][:], ACT.Copy).then_inc(s_zTe, 1)

            def soft_cap(j):
                act.wait_ge(s_gate, j + 1)
                act.activation(rows[ROW_G:ROW_G + HEADS], ps_a[1][ROW_G:ROW_G + HEADS, 0:SEQ], ACT.Tanh,
                               bias=gb[ROW_G:ROW_G + HEADS], scale=1.0 / CAP).then_inc(s_gact, 1)
                act.activation(f_row[:], ps_a[1][ROW_FLOOR:ROW_FLOOR + HEADS, 0:SEQ], ACT.Tanh,
                               bias=gb[ROW_FLOOR:ROW_FLOOR + HEADS], scale=1.0 / CAP).then_inc(s_gact, 1)

            def softplus(j):
                act.preload_act_table_set("natural_log_exp_and_others")
                act.wait_ge(s_gact, 4 * j + 2)
                act.activation(f_row[:], f_row[:], ACT.Exp, scale=-CAP).then_inc(s_gact, 1)
                act.wait_ge(s_gact, 4 * j + 3)
                act.activation(f_row[:], f_row[:], ACT.Ln, bias=1.0).then_inc(s_gact, 1)

            def take_cols(j):
                act.wait_ge(s_colT, j + 1)
                act.activation(cols[:].rearrange("p t r -> p (t r)"), ps_a[1][:, 0:TILES * ROWS], ACT.Copy).then_inc(s_cols, 1)

            def decay(j):
                act.wait_ge(s_cols, j + 1)
                for k, r0 in enumerate((ROW_FLOOR, ROW_CHUNK)):
                    last = act.activation(e_cols[:, :, k, :], cols[:, :, r0:r0 + HEADS], ACT.Exp)
                last.then_inc(s_ecols, 1)
                act.wait_ge(s_mask, TILES * (j + 1))
                reuse(act, s_pv, j)
                for r in range(ROWGRP):
                    d = m_all[:, r:HEADS:ROWGRP, :].rearrange("p c (t q) -> p t c q", q=P)
                    act.activation(smat[:, r], d, ACT.Exp, scale=-1.0).then_inc(s_exp, 1)

            def take_near(j):
                act.wait_ge(s_pv, j + 1)
                act.activation(num[:, 0].rearrange("p h d -> p (h d)"), ps_a[0][:, 0:HEADS * DV], ACT.Copy).then_inc(s_near, 1)

            def take_z2T(j):
                act.wait_ge(s_z2T, j + 1)
                act.activation(z2_hi[:].rearrange("p c t -> p (c t)"), ps_a[0][:], ACT.Copy).then_inc(s_z2hi, 1)

            def silu(i, m):
                act.wait_ge(s_ab, KH * i + m + 1)
                act.activation(silu_a[:, m % 2], ps_f[m % 4][:, 0], ACT.Silu, scale=scl[:, 0, m:m + 1]).then_inc(s_silu, 1)

            def hi_1(i, m):
                act.wait_ge(s_hf, KH * i + m + 1)
                act.activation(h_hi[0][:, m], h_f[:, m % 2], ACT.Copy).then_inc(s_hi1, 1)

            def gelu(i, layer, m):
                n = 2 * KH * i + KH * layer + m
                act.wait_ge(s_mm, n + 1)
                if not (layer == 0 and m < GELU):
                    act.wait_ge(s_lo, n - GELU + 1)
                act.activation(gelu_f[:, m % GELU], ps_f[m % 4][:, 0], ACT.Gelu,
                               scale=scl[:, 2 + layer, m:m + 1]).then_inc(s_gelu, 1)
                act.wait_ge(s_gelu, n + 1)
                act.activation(h_hi[1 - layer][:, m], gelu_f[:, m % GELU], ACT.Copy).then_inc(s_hi, 1)

            def batch(i, ahead, start):
                j = i + LEAD
                for m in range(KH):
                    silu(i, m)
                    if m >= 1:
                        hi_1(i, m - 1)
                    if start and m == 4:
                        take_zT(j)
                hi_1(i, KH - 1)
                if start:
                    soft_cap(j)
                    softplus(j)
                for m in range(KH):
                    gelu(i, 0, m)
                    if start and m == 5:
                        take_cols(j)
                if ahead:
                    take_z2T(i + 1)
                for m in range(KH):
                    gelu(i, 1, m)
                    if start and m == 2:
                        decay(j)
                if start:
                    take_near(j)

            act.wait_ge(s_ready, 1)
            for j in range(LEAD):
                take_zT(j)
                soft_cap(j)
                softplus(j)
                take_cols(j)
                if j == 1:
                    take_z2T(0)
                decay(j)
                take_near(j)
            with act.Fori(0, BATCH - LEAD) as i:
                batch(i, True, True)
            batch(BATCH - 2, True, False)
            batch(BATCH - 1, False, False)

            def general_path(i):
                take_z2T(BATCH + i)
                batch(BATCH + i, False, False)

            if_general(act, general_path)

        @block.vector
        def _(dve):
            count = {}

            def link(chain, base, ins):
                count[chain] = count.get(chain, 0) + 1
                ins.then_inc(chain, 1)
                dve.wait_ge(chain, base + count[chain])

            def rsqrt(chain, base, work, n):
                v, half, prod, y = (work[:, k, 0:n] for k in range(4))
                link(chain, base, dve.tensor_scalar(half.bitcast(I32), v.bitcast(I32), 1, None, ALU.logical_shift_right))
                link(chain, base, dve.tensor_scalar(y.bitcast(I32), half.bitcast(I32), -1.0, float(RSQRT_SEED), ALU.mult, ALU.add))
                for _ in range(3):
                    link(chain, base, dve.tensor_tensor(prod, y, y, ALU.mult))
                    link(chain, base, dve.scalar_tensor_tensor(prod, prod, -0.5, v, ALU.mult, ALU.mult))
                    link(chain, base, dve.scalar_tensor_tensor(y, prod, 1.5, y, ALU.add, ALU.mult))

            def norm_stats(chain, j, src):
                base = NORM_STEPS * j
                count[chain] = 0
                for t in range(TILES):
                    link(chain, base, dve.bn_stats(stats[:, t], src[:, t]))
                dve.sem_inc(s_alone, 1)
                for t in range(TILES):
                    last = dve.bn_aggr(mv[:, t], stats[:, t])
                link(chain, base, last)
                link(chain, base, dve.tensor_scalar(nw[:, 0, 0:TILES], mv[:, :, 1], LN_EPS, None, ALU.add))

            def norm_rsqrt(chain, j):
                rsqrt(chain, NORM_STEPS * j, nw, TILES)
                assert count[chain] == NORM_STEPS

            def norm_apply(j, src, dst, done):
                for t in range(TILES):
                    last = dve.tensor_scalar(dst[:, t], src[:, t], mv[:, t, 0:1], nw[:, 3, t:t + 1], ALU.subtract, ALU.mult)
                last.then_inc(done, 1)
                dve.wait_ge(done, j + 1)

            def norm_1_stats(j):
                dve.wait_ge(s_xin, 16 * j + 16)
                norm_stats(s_norm1, j, x_in)

            def norm_1_apply(j):
                reuse(dve, s_zT, j)
                norm_apply(j, x_in, z, s_z)

            def norm_2_stats(j):
                dve.wait_ge(s_resid, x1_ready(j))
                norm_stats(s_norm2, j, x1)

            def norm_2_apply(j):
                reuse(dve, s_z2T, j)
                norm_apply(j, x1, z2, s_z2)

            def norm_1(j):
                norm_1_stats(j)
                norm_rsqrt(s_norm1, j)
                norm_1_apply(j)

            def norm_2(j):
                norm_2_stats(j)
                norm_rsqrt(s_norm2, j)
                norm_2_apply(j)

            def scans(j):
                dve.wait_ge(s_gact, 4 * j + 4)
                n = SCAN_STEPS * j
                dve.tensor_tensor_scan(f_row[:], f_row[:], f_row[:], 0.0, ALU.add, ALU.max).then_inc(s_scan, 1)
                dve.wait_ge(s_scan, n + 1)
                g = rows[ROW_G:ROW_G + HEADS]
                dve.scalar_tensor_tensor(g, g, CAP, f_row[:], ALU.mult, ALU.add).then_inc(s_scan, 1)
                dve.wait_ge(s_scan, n + 2)
                reuse(dve, s_mst, 16 * j)
                dve.tensor_tensor_scan(m_row[:], g, g, -MASKED, ALU.max, ALU.max).then_inc(s_scan, 1)
                dve.wait_ge(s_scan, n + 3)
                c = m_row[:, P - 1:P]
                dve.tensor_tensor(rows[ROW_FLOOR:ROW_FLOOR + HEADS], f_row[:], m_row[:], ALU.subtract).then_inc(s_scan, 1)
                dve.tensor_scalar(rows[ROW_CHUNK:ROW_CHUNK + HEADS, 0:P], g[:, 0:P], c, None, ALU.subtract).then_inc(s_scan, 1)
                dve.tensor_scalar(rows[ROW_CHUNK:ROW_CHUNK + HEADS, P:SEQ], m_row[:, P:SEQ], -1.0, c, ALU.mult, ALU.add)\
                   .then_inc(s_scan, 1)

            def weigh_scores(j, groups):
                if 0 in groups:
                    dve.wait_ge(s_ecols, j + 1)
                    dve.tensor_scalar(floor[:], e_cols[:, :, 0, :], BACKEND_EPS, None, ALU.add).then_inc(s_floor, 1)
                    dve.wait_ge(s_qk, j + 1)
                for r in groups:
                    dve.wait_ge(s_exp, ROWGRP * j + r + 1)
                    s = smat[:, r].rearrange("p t c q -> p (t c q)")
                    dve.scalar_tensor_tensor(s, ps_a[r][:], SCORE_SCALE, s, ALU.mult, ALU.mult).then_inc(s_smat, 1)

            def take_state(j):
                dve.wait_ge(s_st, j + 1)
                dve.tensor_tensor(state[:], ps_a[2][:, 0:CH * ROWGRP * DV],
                                  head_mask[:].rearrange("p c h d -> p (c h d)"), ALU.mult).then_inc(s_state, 1)

            def take_far(j):
                dve.wait_ge(s_farmm, j + 1)
                u = e_cols[:, 1, 1, :].rearrange("p (h o) -> p h o", o=1).to_broadcast([P, HEADS, DV])
                dve.tensor_tensor(far[:], ps_a[3][:, 0:HEADS * DV].rearrange("p (h d) -> p h d", d=DV), u, ALU.mult)\
                   .then_inc(s_far, 1)
                dve.wait_ge(s_far, j + 1)
                dve.tensor_tensor(num[:, 1], ps_a[1][:, 0:HEADS * DV].rearrange("p (h d) -> p h d", d=DV), far[:], ALU.add)\
                   .then_inc(s_num, 1)

            def mix_divide(j):
                count[s_mix] = 0
                base = MIX_STEPS * j
                n = num[:].rearrange("p t h d -> p (t h) d")
                total = n[:, :, DH]
                dve.wait_ge(s_near, j + 1)
                dve.wait_ge(s_num, j + 1)
                dve.wait_ge(s_floor, j + 1)
                link(s_mix, base, dve.scalar_tensor_tensor(den[:, 0], total, -1.0, total, ALU.mult, ALU.max))
                link(s_mix, base, dve.scalar_tensor_tensor(den[:, 0], den[:, 0], BACKEND_EPS,
                                                           floor[:].rearrange("p t h -> p (t h)"), ALU.add, ALU.max))
                link(s_mix, base, dve.reciprocal(den[:, 1], den[:, 0]))
                per_head = den[:, 1].rearrange("p (h o) -> p h o", o=1).to_broadcast([P, TILES * HEADS, DH])
                link(s_mix, base, dve.tensor_tensor(h_att[:], n[:, :, 0:DH], per_head, ALU.mult))

            def mix_square(j):
                base = MIX_STEPS * j
                link(s_mix, base, dve.tensor_tensor(h_sq[:], h_att[:], h_att[:], ALU.mult))
                link(s_mix, base, dve.tensor_reduce(rms[:, 2], h_sq[:], AX.X, ALU.add))
                link(s_mix, base, dve.tensor_scalar(rms[:, 0], rms[:, 2], 1.0 / DH, RMS_EPS, ALU.mult, ALU.add))

            def mix_rsqrt(j):
                rsqrt(s_mix, MIX_STEPS * j, rms, TILES * HEADS)
                assert count[s_mix] == MIX_STEPS

            def take_z2T(j):
                dve.wait_ge(s_z2hi, j + 1)
                dve.tensor_tensor(z2_lo[:].rearrange("p c t -> p (c t)"), ps_a[0][:],
                                  z2_hi[:].rearrange("p c t -> p (c t)").bitcast(F32), ALU.subtract).then_inc(s_z2lo, 1)

            def swiglu(i, m):
                n = KH * i + m
                dve.wait_ge(s_silu, n + 1)
                if m >= 2:
                    dve.wait_ge(s_lo1, n - 1)
                dve.scalar_tensor_tensor(h_f[:, m % 2], ps_f[m % 4][:, 1], scl[:, 1, m:m + 1], silu_a[:, m % 2],
                                         ALU.mult, ALU.mult).then_inc(s_hf, 1)

            def lo_1(i, m):
                dve.wait_ge(s_hi1, KH * i + m + 1)
                dve.tensor_tensor(h_lo[0][:, m], h_f[:, m % 2], h_hi[0][:, m].bitcast(F32), ALU.subtract).then_inc(s_lo1, 1)

            def lo(i, layer, m):
                dve.wait_ge(s_hi, 2 * KH * i + KH * layer + m + 1)
                dve.tensor_tensor(h_lo[1 - layer][:, m], gelu_f[:, m % GELU], h_hi[1 - layer][:, m].bitcast(F32),
                                  ALU.subtract).then_inc(s_lo, 1)

            def finish(i):
                dve.wait_ge(s_x1f, i + 1)
                for t in range(TILES):
                    dve.wait_ge(s_ymm, TILES * i + t + 1)
                    dve.tensor_tensor(y_out[:, t], ps_f[LAST_BANKS[t]][:, 0], w3s_b[:], ALU.mult).then_inc(s_ysc, 1)
                for t in range(TILES):
                    dve.wait_ge(s_ysc, TILES * (i + 1) + t + 1)
                    dve.tensor_tensor(y_out[:, t], y_out[:, t], x1_ffn[:, t], ALU.add).then_inc(s_y, 1)

            def compare(i):
                dve.wait_ge(s_raw, 16 * i + 16)
                dve.sem_inc(s_alone, 1)
                dve.scalar_tensor_tensor(marks, raw, 1.0, wgt[:, bass.ds(i * COMPARE, COMPARE)].bitcast(F32),
                                         ALU.mult, ALU.not_equal, accum_out=inexact[:, bass.ds(i, 1)]).then_inc(s_inexact, 1)
                dve.wait_ge(s_inexact, i + 1)

            def decide():
                dve.tensor_reduce(inexact_sum[:], inexact[:], AX.X, ALU.add).then_inc(s_inexact_sum, 1)
                dve.wait_ge(s_inexact_all, 1)
                dve.tensor_scalar(general[:], ps_a[0][0:1, 0:1], 0.0, None, ALU.is_gt).then_inc(s_general, 1)

            def batch(i, ahead, start, more, check=True, last=False):
                j = i + LEAD
                for m in range(KH):
                    swiglu(i, m)
                    if m >= 1:
                        lo_1(i, m - 1)
                lo_1(i, KH - 1)
                if ahead:
                    mix_divide(i + 1)
                    mix_square(i + 1)
                    mix_rsqrt(i + 1)
                for m in range(KH):
                    lo(i, 0, m)
                    if start and m == 0:
                        scans(j)
                    if ahead and m == 4:
                        norm_2_stats(i + 1)
                    if ahead and m == 5:
                        norm_rsqrt(s_norm2, i + 1)
                    if ahead and m == 6:
                        norm_2_apply(i + 1)
                if ahead:
                    take_z2T(i + 1)
                for m in range(KH):
                    lo(i, 1, m)
                    if check and m == 0:
                        compare(i)
                    if last and m == 1:
                        decide()
                    if more and m == 2:
                        norm_1_stats(j + 1)
                    if start and m in (3, 4):
                        weigh_scores(j, range(2 * (m - 3), 2 * (m - 2)))
                    if more and m == 5:
                        norm_rsqrt(s_norm1, j + 1)
                    if more and m == 6:
                        norm_1_apply(j + 1)
                    if start and m == 7:
                        take_state(j)
                        take_far(j)
                finish(i)

            dve.sem_inc(s_ysc, TILES)
            dve.memset(rows[:], 0.0).then_inc(s_cleared, 1)
            dve.memset(gw[:], 0.0).then_inc(s_cleared, 1)
            dve.wait_ge(s_cleared, 2)
            dve.wait_ge(s_ident, 6)
            norm_1(0)
            dve.wait_ge(s_const, 16 * 6)
            for k, r0 in enumerate((ROW_G, ROW_FLOOR)):
                w = gw_in[:, :, k * HEADS:(k + 1) * HEADS]
                dve.tensor_copy(gw[:, 0:CH, r0:r0 + HEADS], w[:, 0:CH])
                dve.tensor_tensor(gw[:, CH:2 * CH, r0:r0 + HEADS], w[:, CH:2 * CH], w[:, 2 * CH:3 * CH], ALU.add)
            dve.tensor_scalar(gb[:], gb_in[:], 1.0 / CAP, None, ALU.mult)
            dve.tensor_scalar(gain_b[:], gain_b[:], 1.0, None, ALU.add).then_inc(s_ready, 1)
            dve.wait_ge(s_ready, 1)
            scans(0)
            norm_1(1)
            weigh_scores(0, range(ROWGRP))
            take_state(0)
            take_far(0)
            mix_divide(0)
            mix_square(0)
            mix_rsqrt(0)
            scans(1)
            norm_2(0)
            take_z2T(0)
            norm_1(2)
            weigh_scores(1, range(ROWGRP))
            take_state(1)
            take_far(1)
            dve.wait_ge(s_wgt, 16 * UNITS // PER_LOAD)
            with dve.Fori(0, BATCH - LEAD - 1) as i:
                batch(i, True, True, True)
            batch(BATCH - LEAD - 1, True, True, False)
            batch(BATCH - 2, True, False, False)
            batch(BATCH - 1, False, False, False, last=True)

            def general_path(i):
                g = BATCH + i
                dve.wait_ge(s_x1in, 16 * i + 16)
                norm_stats(s_norm2, g, x1)
                norm_rsqrt(s_norm2, g)
                norm_2_apply(g)
                take_z2T(g)
                batch(g, False, False, False, check=False)

            if_general(dve, general_path)

        @block.tensor
        def _(pe):
            def turn(src, done):
                for c in range(CH):
                    for t in range(TILES):
                        col = c * SEQ + t * P
                        last = pe.transpose(ps_a[0][:, col:col + P], src[:, t, c * P:(c + 1) * P], ident[:])
                last.then_inc(done, 1)

            def turn_z(j):
                pe.wait_ge(s_z, j + 1)
                reuse(pe, s_near, j)
                turn(z, s_zT)

            def turn_z2(j):
                pe.wait_ge(s_z2, j + 1)
                turn(z2, s_z2T)

            def gates(j):
                pe.wait_ge(s_zTe, j + 1)
                pe.wait_ge(s_ctxT, 16 * j + 16)
                reuse(pe, s_num, j)
                for c in range(CH):
                    pe.matmul(ps_a[1][0:GATE_COLS, 0:SEQ], gw[:, CH + c], ctxT[:, c], start=(c == 0), stop=False)
                for c in range(CH):
                    last = pe.matmul(ps_a[1][0:GATE_COLS, 0:SEQ], gw[:, c], zT[:, c], start=False, stop=(c == CH - 1))
                last.then_inc(s_gate, 1)

            def turn_rows(j):
                pe.wait_ge(s_scan, SCAN_STEPS * j + SCAN_STEPS)
                for t in range(TILES):
                    last = pe.transpose(ps_a[1][:, t * ROWS:(t + 1) * ROWS], rows[:, t * P:(t + 1) * P], ident[0:ROWS, 0:ROWS])
                last.then_inc(s_colT, 1)

            def scores(j):
                pe.wait_ge(s_cols, j + 1)
                reuse(pe, s_z2lo, j)
                for t in range(TILES):
                    for c in range(CH):
                        for r in range(ROWGRP):
                            d = slice(r * DH, (r + 1) * DH)
                            col = (t * CH + c) * P
                            last = pe.matmul(ps_a[r][:, col:col + P], ctxT[d, c, t * P:(t + 1) * P],
                                             zT[d, c, t * P:(t + 1) * P], start=True, stop=True)
                last.then_inc(s_qk, 1)

            def make_state(j):
                pe.wait_ge(s_kwt, j + 1)
                pe.wait_ge(s_smat, ROWGRP * j + 3)
                for c in range(CH):
                    h = slice(c * ROWGRP, (c + 1) * ROWGRP)
                    last = pe.matmul(ps_a[2][:, c * ROWGRP * DV:(c + 1) * ROWGRP * DV], k_wt[:, h, :], v_aug[:, 0, h, :],
                                     start=True, stop=True)
                last.then_inc(s_st, 1)

            def values(j):
                pe.wait_ge(s_smat, ROWGRP * j + ROWGRP)
                pe.wait_ge(s_v, 16 * j + 16)
                for t in range(TILES):
                    for h in range(HEADS):
                        last = pe.matmul(ps_a[t][:, h * DV:(h + 1) * DV], smat[:, h % ROWGRP, t, h // ROWGRP, :],
                                         v_aug[:, t, h, :], start=True, stop=True)
                last.then_inc(s_pv, 1)

            def read_state(j):
                pe.wait_ge(s_state, j + 1)
                for c in range(CH):
                    part = slice(c * ROWGRP * DV, (c + 1) * ROWGRP * DV)
                    last = pe.matmul(ps_a[3][:, part], zT[:, c, P:SEQ], state[:, part], start=True, stop=True)
                last.then_inc(s_farmm, 1)

            def columns(u, col, width, as_is):
                if as_is:
                    slot = ORDER.index(u) % STAGE
                    return stage[:, slot * UNIT + col:slot * UNIT + col + width]
                return wgt[:, u * UNIT + col:u * UNIT + col + width]

            def moving(a, as_is):
                return a.bitcast(F32) if as_is else a

            def swiglu(i, m, as_is):
                if m in LAST_BANKS:
                    pe.wait_ge(s_ysc, TILES * i + LAST_BANKS.index(m) + 1)
                if m >= 4:
                    pe.wait_ge(s_hf, KH * i + m - 3)
                per = KH // N_W1
                for half, base in enumerate((UNIT_W1, UNIT_W2)):
                    if as_is and m % per == 0:
                        pe.wait_ge(*unit_landed(i - BATCH, base + m // per))
                    for c in range(CH):
                        w = columns(base + m // per, (m % per * CH + c) * P, P, as_is)
                        pe.matmul(ps_f[m % 4][:, half], w, moving(z2_hi[:, c], as_is), start=(c == 0), stop=False)
                        last = pe.matmul(ps_f[m % 4][:, half], w, moving(z2_lo[:, c], as_is), start=False, stop=(c == CH - 1))
                last.then_inc(s_ab, 1)

            def hidden(i, layer, m, ks, as_is):
                group = KH * layer + m
                unit = UNIT_H1 + group
                if ks[0] == 0:
                    if as_is:
                        pe.wait_ge(*unit_landed(i - BATCH, unit))
                    if group >= 4:
                        pe.wait_ge(s_gelu, 2 * KH * i + group - 3)
                for k in ks:
                    if layer == 0:
                        if m < 2:
                            pe.wait_ge(s_lo1, KH * i + max(k + 1, m + 5))
                        elif m < 4 and k == 0:
                            pe.wait_ge(s_lo1, KH * i + KH)
                    elif m < 2:
                        pe.wait_ge(s_lo, 2 * KH * i + k + 1)
                    w = columns(unit, k * P, P, as_is)
                    pe.matmul(ps_f[m % 4][:, 0], w, moving(h_hi[layer][:, k], as_is), start=(k == 0), stop=False)
                    last = pe.matmul(ps_f[m % 4][:, 0], w, moving(h_lo[layer][:, k], as_is), start=False, stop=(k == KH - 1))
                if ks[-1] == KH - 1:
                    last.then_inc(s_mm, 1)

            def hidden_layer(i, layer, as_is, after):
                for m in range(2):
                    hidden(i, layer, m, range(KH - 1), as_is)
                after(-1)
                for m in range(2):
                    hidden(i, layer, m, range(KH - 1, KH), as_is)
                    after(m)
                for m in range(2, KH):
                    hidden(i, layer, m, range(KH), as_is)
                    after(m)

            def project(i, as_is):
                per = UNIT // DIM

                def part(t, ks):
                    for k in ks:
                        if as_is and k % per == 0:
                            pe.wait_ge(*unit_landed(i - BATCH, UNIT_W3 + k // per))
                        pe.wait_ge(s_lo, 2 * KH * i + KH + max(k + 1, LAST_BANKS[t] + 5))
                        w = columns(UNIT_W3 + k // per, k % per * DIM, DIM, as_is)
                        pe.matmul(ps_f[LAST_BANKS[t]][:, 0], moving(h_hi[0][:, k, t * P:(t + 1) * P], as_is), w, start=(k == 0), stop=False)
                        last = pe.matmul(ps_f[LAST_BANKS[t]][:, 0], moving(h_lo[0][:, k, t * P:(t + 1) * P], as_is), w, start=False,
                                         stop=(k == KH - 1))
                    return last

                for t in range(TILES):
                    part(t, range(KH - 1))
                for t in range(TILES):
                    part(t, range(KH - 1, KH)).then_inc(s_ymm, 1)

            def count_inexact():
                pe.wait_ge(s_inexact_sum, 1)
                pe.matmul(ps_a[0][0:1, 0:1], inexact_sum[:], ones[:], start=True, stop=True).then_inc(s_inexact_all, 1)

            def batch(i, ahead, start, as_is=False, last=False):
                j = i + LEAD
                pe.wait_ge(s_z2lo, i + 1)
                for m in range(KH):
                    swiglu(i, m, as_is)
                    if start and m == 2:
                        turn_z(j)
                if start:
                    gates(j)

                def after_2(m):
                    if start and m == 4:
                        turn_rows(j)

                def after_3(m):
                    if ahead and m == -1:
                        turn_z2(i + 1)
                    if start and m == 2:
                        scores(j)
                    if last and m == 3:
                        count_inexact()
                    if start and m == 6:
                        make_state(j)
                    if start and m == 7:
                        values(j)
                        read_state(j)

                hidden_layer(i, 0, as_is, after_2)
                hidden_layer(i, 1, as_is, after_3)
                project(i, as_is)

            def attend(j):
                scores(j)
                make_state(j)
                values(j)
                read_state(j)

            pe.wait_ge(s_ident, 6)
            pe.wait_ge(s_cleared, 2)
            turn_z(0)
            pe.wait_ge(s_ready, 1)
            gates(0)
            turn_rows(0)
            attend(0)
            turn_z(1)
            gates(1)
            turn_rows(1)
            turn_z2(0)
            attend(1)
            pe.wait_ge(s_wgt, 16 * UNITS // PER_LOAD)
            with pe.Fori(0, BATCH - LEAD) as i:
                batch(i, True, True)
            batch(BATCH - 2, True, False)
            batch(BATCH - 1, False, False, last=True)

            def general_path(i):
                turn_z2(BATCH + i)
                batch(BATCH + i, False, False, as_is=True)

            if_general(pe, general_path)


def kernel(x, ctx_1024, L0_xattn_ifgate_w, L0_xattn_ifgate_b, L0_xattn_outnorm_w, L0_ffn_w1_w, L0_ffn_w1_s, L0_ffn_w2_w,
           L0_ffn_w2_s, L0_ffn_h1_w, L0_ffn_h1_s, L0_ffn_h2_w, L0_ffn_h2_s, L0_ffn_w3_w, L0_ffn_w3_s):
    import concourse.bacc as bacc
    from concourse.bass_utils import run_bass_kernel_spmd

    def tok(a):
        return np.ascontiguousarray(np.asarray(a).reshape(BATCH, TILES, P, DIM).transpose(0, 2, 1, 3))

    ctx = np.asarray(ctx_1024)
    v_aug = np.ones((BATCH, P, TILES, HEADS, DV), np.float32)
    v_aug[..., 0:DH] = tok(ctx).reshape(BATCH, P, TILES, HEADS, DH)
    ctx_t = np.ascontiguousarray(ctx.reshape(BATCH, SEQ, CH, P).transpose(0, 3, 2, 1))

    def up(w):
        return np.asarray(w).reshape(N_W1, KH // N_W1, P, CH, P).transpose(0, 4, 1, 3, 2).reshape(N_W1, P, UNIT)

    def square(w):
        return np.asarray(w).reshape(KH, P, KH, P).transpose(0, 3, 2, 1).reshape(KH, P, UNIT)

    def down(w):
        n = KH * DIM // UNIT
        return np.asarray(w).reshape(DIM, n, KH // n, P).transpose(1, 3, 2, 0).reshape(n, P, UNIT)

    w_units = np.concatenate([up(L0_ffn_w1_w), up(L0_ffn_w2_w), square(L0_ffn_h1_w), square(L0_ffn_h2_w),
                              down(L0_ffn_w3_w)])
    w_cols = np.ascontiguousarray(w_units.transpose(1, 0, 2).reshape(P, COLS))
    scales = np.ascontiguousarray(np.stack([np.asarray(s).reshape(KH, P) for s in
                                            (L0_ffn_w1_s, L0_ffn_w2_s, L0_ffn_h1_s, L0_ffn_h2_s)]).transpose(2, 0, 1))
    gate_w = np.ascontiguousarray(np.asarray(L0_xattn_ifgate_w).reshape(2 * HEADS, 3 * CH, P).transpose(2, 1, 0))
    arrays = {
        "x": tok(x), "ctx_tok": v_aug, "ctx_t": ctx_t, "gate_w": gate_w,
        "gate_b": np.ascontiguousarray(np.asarray(L0_xattn_ifgate_b).reshape(2, HEADS, 1)),
        "outnorm_w": np.ascontiguousarray(np.asarray(L0_xattn_outnorm_w).reshape(1, DIM)),
        "w_cols": w_cols, "scales": scales, "w3_s": np.ascontiguousarray(np.asarray(L0_ffn_w3_s).reshape(1, DIM)),
    }
    nc = bacc.Bacc("TRN2", target_bir_lowering=False, num_devices=1)
    args = {n: nc.dram_tensor(n, a.shape, F32, kind="ExternalInput").ap() for n, a in arrays.items()}
    out = nc.dram_tensor("out", (BATCH, P, TILES, DIM), F32, kind="ExternalOutput").ap()
    build(nc, out=out, **args)
    got = run_bass_kernel_spmd(nc, [arrays], core_ids=[0]).results[0]["out"]
    return np.ascontiguousarray(np.asarray(got).transpose(0, 2, 1, 3).reshape(BATCH, SEQ, DIM))
```

```python
from contextlib import ExitStack

import numpy as np

import concourse.bass as bass
from concourse import mybir

ALU = mybir.AluOpType
ACT = mybir.ActivationFunctionType
AX = mybir.AxisListType
F32 = mybir.dt.float32
F32R = mybir.dt.float32r
BF16 = mybir.dt.bfloat16
I32 = mybir.dt.int32

P = 128
BATCH, SEQ, DIM = 16, 256, 256
HEADS, DH = 8, 32
HID = 1024
TILES = SEQ // P
CH = DIM // P
KH = HID // P
ROWGRP = P // DH
DV = DH + 1
CAP = 15.0
SCORE_SCALE = float(1.0 / np.sqrt(DH))
BACKEND_EPS, RMS_EPS, LN_EPS = 5e-05, 1e-06, 1e-05
MASKED = 1e30
RSQRT_SEED = 0x5F3759DF

UNIT = 1024
N_W1 = CH * HID // UNIT
UNIT_W1, UNIT_W2 = 0, N_W1
UNIT_H1 = 2 * N_W1
UNIT_H2 = UNIT_H1 + KH
UNIT_W3 = UNIT_H2 + KH
UNITS = UNIT_W3 + KH * DIM // UNIT
COLS = UNITS * UNIT
LOADS = ((0, 2), (0, 2), (1, 2), (1, 2), (1, 1), (1, 3), (2, 4), (2, 4), (3, 2))
LAYERS = 4
GELU = 4
STAGE = 4
COMPARE = COLS // BATCH

ROW_G, ROW_FLOOR, ROW_CHUNK = 0, 32, 64
ROWS = ROW_CHUNK + HEADS
GATE_COLS = ROW_FLOOR + HEADS
ROW_LOW = 64
SPLIT_COLS = ROW_LOW + GATE_COLS

RSQRT_STEPS = 11
NORM_STEPS = TILES + 2 + RSQRT_STEPS
MIX_STEPS = 7 + RSQRT_STEPS
GATE_STEPS = 3
SCAN_STEPS = 6
RESIDUAL_STEPS = 3

LAST_BANKS = (2, 3)

LEAD = 2


def build(nc, x, ctx_tok, ctx_t, gate_w, gate_b, outnorm_w, w_cols, scales, w3_s, out):
    with ExitStack() as stack:
        def sb(name, shape, dt=F32):
            return stack.enter_context(nc.sbuf_tensor(name, shape, dt))

        def sem(name):
            return stack.enter_context(nc.semaphore(name))

        x1_kept = nc.dram_tensor("x1_kept", [BATCH, P, TILES, DIM], F32, kind="Internal").ap()
        m_rows = nc.dram_tensor("m_rows", [HEADS, SEQ], F32, kind="Internal").ap()

        wgt = sb("wgt", [P, COLS], F32R)
        stage = sb("stage", [P, STAGE * UNIT])
        raw = stage[:, 0:COMPARE]
        marks = stage[:, COMPARE:COMPARE + COMPARE // 2].bitcast(BF16)
        h_hi = [sb(f"h_hi{n}", [P, KH, SEQ], F32R) for n in range(2)]
        h_lo = [sb(f"h_lo{n}", [P, KH, SEQ], F32R) for n in range(2)]
        z2_hi = sb("z2_hi", [P, CH, SEQ], F32R)
        z2_lo = sb("z2_lo", [P, CH, SEQ], F32R)
        keys_hi, keys_lo = h_hi[1][:, 0:CH], h_lo[1][:, 0:CH]
        normed_hi, normed_lo = h_hi[1][:, CH:2 * CH], h_lo[1][:, CH:2 * CH]
        silu_a = sb("silu_a", [P, 2, SEQ])
        h_f = sb("h_f", [P, 2, SEQ])
        gelu_f = sb("gelu_f", [P, GELU, SEQ])
        scl = sb("scl", [P, 4, KH])
        w3s_b = sb("w3s_b", [P, DIM])
        gain_b = sb("gain_b", [P, DIM])
        ident = sb("ident", [P, P])
        head_mask = sb("head_mask", [P, CH, ROWGRP, DV])
        gw_in = sb("gw_in", [P, 3 * CH, 2 * HEADS])
        gw = sb("gw", [P, 2 * CH, GATE_COLS])
        gw_split = sb("gw_split", [P, 2 * CH, SPLIT_COLS], F32R)
        gate_low = sb("gate_low", [GATE_COLS, SEQ])
        gate_sum = sb("gate_sum", [GATE_COLS, SEQ])
        gb_in = sb("gb_in", [GATE_COLS, 1])
        gb = sb("gb", [GATE_COLS, 1])

        x_in = sb("x_in", [P, TILES, DIM])
        x1 = sb("x1", [P, TILES, DIM])
        x1_ffn = sb("x1_ffn", [P, TILES, DIM])
        x_res = sb("x_res", [P, TILES, DIM])
        y_out = sb("y_out", [P, TILES, DIM])
        ctxT = sb("ctxT", [P, CH, SEQ])
        v_aug = sb("v_aug", [P, TILES, HEADS, DV])
        k_wt = sb("k_wt", [P, HEADS, DH])
        z = sb("z", [P, TILES, DIM])
        z2 = sb("z2", [P, TILES, DIM])
        zT = sb("zT", [P, CH, SEQ])
        rows = sb("rows", [ROWS, SEQ])
        f_row = sb("f_row", [HEADS, SEQ])
        m_row = sb("m_row", [HEADS, SEQ])
        m_all = sb("m_all", [P, HEADS, SEQ])
        cols = sb("cols", [P, TILES, ROWS])
        e_cols = sb("e_cols", [P, TILES, 2, HEADS])
        floor = sb("floor", [P, TILES, HEADS])
        smat = sb("smat", [P, ROWGRP, TILES, CH, P])
        state = sb("state", [P, CH * ROWGRP * DV])
        num = sb("num", [P, TILES, HEADS, DV])
        far = sb("far", [P, HEADS, DV])
        h_att = sb("h_att", [P, TILES * HEADS, DH])
        h_sq = sb("h_sq", [P, TILES * HEADS, DH])
        stats = sb("stats", [P, TILES, 6])
        mv = sb("mv", [P, TILES, 2])
        nw = sb("nw", [P, 4, TILES * HEADS])
        rms = sb("rms", [P, 4, TILES * HEADS])
        inexact = sb("inexact", [P, BATCH])
        inexact_sum = sb("inexact_sum", [P, 1])
        general = sb("general", [1, 1], I32)
        ones = sb("ones", [P, 1])
        den = sb("den", [P, 2, TILES * HEADS])

        ps_f = [stack.enter_context(nc.psum_tensor(f"ps_f{n}", [P, 2, SEQ], F32)) for n in range(4)]
        ps_a = [stack.enter_context(nc.psum_tensor(f"ps_a{n}", [P, 512], F32)) for n in range(4)]

        s_alone = sem("s_alone")
        s_gb0 = sem("s_gb0")
        s_cleared = sem("s_cleared")
        s_const = sem("s_const")
        s_layer_const = sem("s_layer_const")
        s_ready = sem("s_ready")
        s_ident = sem("s_ident")
        s_wgt = [sem(f"s_wgt{n}") for n in range(LAYERS)]
        s_raw = sem("s_raw")
        s_inexact = sem("s_inexact")
        s_inexact_sum = sem("s_inexact_sum")
        s_inexact_all = sem("s_inexact_all")
        s_general = sem("s_general")
        s_unit = [sem(f"s_unit{n}") for n in range(STAGE)]
        s_x1in = sem("s_x1in")
        s_xin = sem("s_xin")
        s_xin_early = sem("s_xin_early")
        s_ctxT = sem("s_ctxT")
        s_ctxT_early = sem("s_ctxT_early")
        s_v = sem("s_v")
        s_norm1 = sem("s_norm1")
        s_z = sem("s_z")
        s_xres = sem("s_xres")
        s_zT = sem("s_zT")
        s_zTe = sem("s_zTe")
        s_gw_split = sem("s_gw_split")
        s_keys_hi = sem("s_keys_hi")
        s_keys_lo = sem("s_keys_lo")
        s_zhi = sem("s_zhi")
        s_zlo = sem("s_zlo")
        s_gate = sem("s_gate")
        s_gate_low = sem("s_gate_low")
        s_gate_sum = sem("s_gate_sum")
        s_gact = sem("s_gact")
        s_scan = sem("s_scan")
        s_mst = sem("s_mst")
        s_mall = sem("s_mall")
        s_decay = sem("s_decay")
        s_decay_early = sem("s_decay_early")
        s_mask = sem("s_mask")
        s_colT = sem("s_colT")
        s_cols = sem("s_cols")
        s_ecols = sem("s_ecols")
        s_floor = sem("s_floor")
        s_exp = sem("s_exp")
        s_qk = sem("s_qk")
        s_smat = sem("s_smat")
        s_kwt = sem("s_kwt")
        s_st = sem("s_st")
        s_state = sem("s_state")
        s_pv = sem("s_pv")
        s_farmm = sem("s_farmm")
        s_far = sem("s_far")
        s_near = sem("s_near")
        s_num = sem("s_num")
        s_mix = sem("s_mix")
        s_resid = sem("s_resid")
        s_x1kept = sem("s_x1kept")
        s_norm2 = sem("s_norm2")
        s_z2 = sem("s_z2")
        s_z2T = sem("s_z2T")
        s_z2hi = sem("s_z2hi")
        s_z2lo = sem("s_z2lo")
        s_x1f = sem("s_x1f")
        s_ab = sem("s_ab")
        s_silu = sem("s_silu")
        s_hf = sem("s_hf")
        s_hi1 = sem("s_hi1")
        s_lo1 = sem("s_lo1")
        s_mm = sem("s_mm")
        s_gelu = sem("s_gelu")
        s_hi = sem("s_hi")
        s_lo = sem("s_lo")
        s_ymm = sem("s_ymm")
        s_ysc = sem("s_ysc")
        s_y = sem("s_y")
        s_out = sem("s_out")

        def early(j):
            return isinstance(j, int) and j == 1

        def tokens(j):
            return y_out[:] if early(j) else x_in[:]

        def keys(j):
            return h_f[:] if early(j) else ctxT[:]

        def normed(j):
            return gelu_f[:, 0:CH] if early(j) else zT[:]

        def maxima(j):
            return stage[:, 0:HEADS * SEQ].rearrange("p (h t) -> p h t", h=HEADS) if early(j) else m_all[:]

        def bank(j, n):
            return ps_f[n][:].rearrange("p a t -> p (a t)") if early(j) else ps_a[n][:]

        def plain(j):
            return isinstance(j, int) and j < LEAD

        def half_groups(half):
            return range(half * ROWGRP // 2, (half + 1) * ROWGRP // 2)

        def x1_ready(j):
            return RESIDUAL_STEPS * (j + 1)

        def reuse(eng, semaphore, value):
            if not (isinstance(value, int) and value == 0):
                eng.wait_ge(semaphore, value)

        ORDER = [u for n in range(N_W1) for u in (UNIT_W1 + n, UNIT_W2 + n)] + list(range(UNIT_H1, UNITS))
        PER_SLOT = [len(range(n, UNITS, STAGE)) for n in range(STAGE)]

        def weights_in(eng, layer):
            eng.wait_ge(s_wgt[layer], 16 * sum(n == layer for n, _ in LOADS))

        def unit_landed(i, u):
            q = ORDER.index(u)
            return s_unit[q % STAGE], 16 * (PER_SLOT[q % STAGE] * i + q // STAGE + 1)

        def if_general(eng, path):
            eng.wait_ge(s_general, 1)
            with eng.If(eng.value_load(general[0:1, 0:1]) != 0):
                with eng.Fori(0, BATCH) as i:
                    path(i)

        block = stack.enter_context(nc.Block())

        def landed(j, semaphore, its_own):
            return (its_own, 16) if early(j) else (semaphore, 16 if isinstance(j, int) and j == 0 else 16 * j)

        def last_in_place(j):
            return j if not isinstance(j, int) or j > LEAD else (0, 0, 1)[j]

        def load_x(eng, j):
            reuse(eng, s_xres, last_in_place(j))
            eng.sem_inc(s_alone, 1)
            eng.dma_start(tokens(j), x[bass.ds(j, 1)].rearrange("b p t d -> (b p) t d"))\
               .then_inc(landed(j, s_xin, s_xin_early)[0], 16)

        def shift(eng, j, t):
            part = maxima(j)[:, :, t * P:(t + 1) * P]
            g = cols[:, t, ROW_G:ROW_G + HEADS].rearrange("p (h o) -> p h o", o=1).to_broadcast([P, HEADS, P])
            return eng.tensor_tensor(part, part, g, ALU.subtract)

        def residual(eng, j):
            eng.wait_ge(s_mix, MIX_STEPS * (j + 1))
            rr = rms[:, 3].rearrange("p (h o) -> p h o", o=1).to_broadcast([P, TILES * HEADS, DH])
            eng.tensor_tensor(h_att[:], h_att[:], rr, ALU.mult).then_inc(s_resid, 1)
            eng.wait_ge(s_resid, RESIDUAL_STEPS * j + 1)
            for t in range(TILES):
                h = h_att[:, t * HEADS:(t + 1) * HEADS].rearrange("p h d -> p (h d)")
                last = eng.tensor_tensor(h, h, gain_b[:], ALU.mult)
            last.then_inc(s_resid, 1)
            eng.wait_ge(s_resid, RESIDUAL_STEPS * j + 2)
            reuse(eng, s_x1f, j)
            eng.sem_inc(s_alone, 1)
            reuse(eng, s_x1kept, 16 * j)
            eng.sem_inc(s_alone, 1)
            eng.tensor_tensor(x1[:].rearrange("p t d -> p (t d)"), h_att[:].rearrange("p h d -> p (h d)"),
                               x_res[:].rearrange("p t d -> p (t d)"), ALU.add).then_inc(s_resid, 1)

        def load_ctxT(eng, j):
            reuse(eng, s_qk, 2 * last_in_place(j))
            eng.sem_inc(s_alone, 1)
            eng.dma_start(keys(j), ctx_t[bass.ds(j, 1)].rearrange("b p c t -> (b p) c t"))\
               .then_inc(landed(j, s_ctxT, s_ctxT_early)[0], 16)

        def load_v(eng, j):
            reuse(eng, s_pv, TILES * j)
            eng.sem_inc(s_alone, 1)
            eng.dma_start(v_aug[:], ctx_tok[bass.ds(j, 1)].rearrange("b p t h d -> (b p) t h d")).then_inc(s_v, 16)

        def spread_max(eng, j):
            eng.wait_ge(s_scan, SCAN_STEPS * j + 3)
            eng.sem_inc(s_alone, 1)
            reuse(eng, s_exp, ROWGRP * last_in_place(j))
            eng.sem_inc(s_alone, 1)
            reuse(eng, s_mall, 16 * j)
            eng.sem_inc(s_alone, 1)
            eng.dma_start(m_rows, m_row[:]).then_inc(s_mst, 16)
            eng.wait_ge(s_mst, 16 * j + 16)
            eng.sem_inc(s_alone, 1)
            eng.dma_start(maxima(j), m_rows.rearrange("(o h) t -> o h t", o=1).to_broadcast([P, HEADS, SEQ])).then_inc(s_mall, 16)

        def keep_x1(eng, j):
            eng.wait_ge(s_resid, x1_ready(j))
            eng.sem_inc(s_alone, 1)
            eng.dma_start(x1_kept[bass.ds(j, 1)].rearrange("b p t d -> (b p) t d"), x1[:]).then_inc(s_x1kept, 16)

        def load_raw(eng, i):
            reuse(eng, s_inexact, i)
            eng.sem_inc(s_alone, 1)
            eng.dma_start(raw, w_cols[:, bass.ds(i * COMPARE, COMPARE)]).then_inc(s_raw, 16)

        @block.sync
        def _(sp):
            load_x(sp, 0)
            sp.dma_start(gw_in[:], gate_w).then_inc(s_const, 16)
            sp.wait_ge(s_gb0, 1)
            sp.dma_start(gb_in[ROW_G:ROW_G + HEADS], gate_b[0]).then_inc(s_const, 16)
            sp.dma_start(gb_in[ROW_FLOOR:ROW_FLOOR + HEADS], gate_b[1]).then_inc(s_const, 16)
            sp.dma_start(gain_b[:], outnorm_w.to_broadcast([P, DIM])).then_inc(s_const, 16)
            load_ctxT(sp, 0)
            load_x(sp, 1)
            load_ctxT(sp, 1)
            load_v(sp, 0)
            sp.dma_start(scl[:], scales).then_inc(s_layer_const, 16)
            sp.dma_start(w3s_b[:], w3_s.to_broadcast([P, DIM])).then_inc(s_layer_const, 16)
            load_x(sp, 2)
            spread_max(sp, 0)
            spread_max(sp, 1)
            load_v(sp, 1)
            load_ctxT(sp, 2)
            sp.wait_ge(s_exp, ROWGRP * LEAD)
            load_raw(sp, 0)
            keep_x1(sp, 0)
            load_v(sp, 2)
            with sp.Fori(0, BATCH - LEAD - 1) as i:
                spread_max(sp, i + LEAD)
                keep_x1(sp, i + 1)
                load_x(sp, i + LEAD + 1)
                load_raw(sp, i + 1)
                load_ctxT(sp, i + LEAD + 1)
                load_v(sp, i + LEAD + 1)
            spread_max(sp, BATCH - 1)
            for i in range(BATCH - LEAD - 1, BATCH - 1):
                keep_x1(sp, i + 1)
                load_raw(sp, i + 1)
            sp.wait_ge(s_mst, 16 * BATCH)
            sp.wait_ge(s_x1kept, 16 * BATCH)

            def general_path(i):
                g = BATCH + i
                sp.wait_ge(s_x1f, g)
                sp.sem_inc(s_alone, 1)
                sp.wait_ge(s_z2, g)
                sp.sem_inc(s_alone, 1)
                sp.dma_start(x1[:], x1_kept[bass.ds(i, 1)].rearrange("b p t d -> (b p) t d")).then_inc(s_x1in, 16)
                for q, u in enumerate(ORDER):
                    if q < STAGE:
                        sp.wait_ge(s_ymm, TILES * g)
                    elif q < 2 * STAGE:
                        sp.wait_ge(s_ab, KH * g + (KH // 2 if q < STAGE + 2 else KH))
                    else:
                        sp.wait_ge(s_mm, 2 * KH * g + q - 2 * STAGE + 1)
                    sp.sem_inc(s_alone, 1)
                    sp.dma_start(stage[:, q % STAGE * UNIT:(q % STAGE + 1) * UNIT], w_cols[:, u * UNIT:(u + 1) * UNIT])\
                      .then_inc(s_unit[q % STAGE], 16)

            if_general(sp, general_path)

        @block.gpsimd
        def _(pool):
            pool.memset(gb_in[:], 0.0).then_inc(s_gb0, 1)
            pool.memset(ident[:], 0.0).then_inc(s_ident, 1)
            pool.memset(head_mask[:], SCORE_SCALE).then_inc(s_ident, 1)
            pool.wait_ge(s_ident, 2)
            pool.affine_select(out=ident[:], in_=ident[:], compare_op=ALU.not_equal, fill=1.0, base=0,
                               pattern=[[-1, P]], channel_multiplier=1).then_inc(s_ident, 1)
            pool.affine_select(out=head_mask[:], in_=head_mask[:], compare_op=ALU.is_ge, fill=0.0, base=0,
                               pattern=[[0, CH], [-DH, ROWGRP], [0, DV]], channel_multiplier=1).then_inc(s_ident, 1)
            pool.wait_ge(s_ident, 4)
            pool.affine_select(out=head_mask[:], in_=head_mask[:], compare_op=ALU.is_ge, fill=0.0, base=DH - 1,
                               pattern=[[0, CH], [DH, ROWGRP], [0, DV]], channel_multiplier=-1).then_inc(s_ident, 1)

            def mask_future(j, t):
                part = maxima(j)[:, :, t * P:(t + 1) * P]
                pool.affine_select(out=part, in_=part, compare_op=ALU.is_ge, fill=MASKED, base=0,
                                   pattern=[[0, HEADS], [1, P]], channel_multiplier=-1).then_inc(s_mask, 1)

            def mask_decay(j):
                for t in range(TILES):
                    pool.wait_ge(s_decay_early, t + 1)
                    mask_future(j, t)

            def decay_exponents(j):
                pool.wait_ge(s_mall, 16 * j + 16)
                pool.sem_inc(s_alone, 1)
                pool.wait_ge(s_cols, j + 1)
                pool.sem_inc(s_alone, 1)
                for t in range(TILES):
                    shift(pool, j, t).then_inc(s_decay, 1)
                    pool.wait_ge(s_decay, TILES * (j - 1) + t + 1)
                    pool.sem_inc(s_alone, 1)
                    mask_future(j, t)

            def weigh_keys(j):
                pool.wait_ge(s_ecols, j + 1)
                pool.wait_ge(s_v, 16 * j + 16)
                reuse(pool, s_st, j)
                w = e_cols[:, 0, 1, :].rearrange("p (h o) -> p h o", o=1).to_broadcast([P, HEADS, DH])
                pool.tensor_tensor(k_wt[:], v_aug[:, 0, :, 0:DH], w, ALU.mult).then_inc(s_kwt, 1)

            def split_keys_low(j):
                pool.wait_ge(s_keys_hi, j - LEAD + 1)
                pool.tensor_tensor(keys_lo, ctxT[:], keys_hi.bitcast(F32), ALU.subtract).then_inc(s_keys_lo, 1)

            def split_normed_low(j):
                pool.wait_ge(s_zhi, j - LEAD + 1)
                pool.tensor_tensor(normed_lo, zT[:], normed_hi.bitcast(F32), ALU.subtract).then_inc(s_zlo, 1)

            def keep_tokens(j):
                pool.wait_ge(s_z, j + 1)
                reuse(pool, s_resid, x1_ready(j - 1) if not isinstance(j, int) or j else 0)
                pool.sem_inc(s_alone, 1)
                pool.tensor_copy(x_res[:], tokens(j)).then_inc(s_xres, 1)

            def keep_residual(i):
                pool.sem_inc(s_alone, 1)
                pool.tensor_copy(x1_ffn[:], x1[:]).then_inc(s_x1f, 1)

            def store(i, b):
                pool.wait_ge(s_y, TILES * i + TILES)
                pool.sem_inc(s_alone, 1)
                pool.dma_start(out[bass.ds(b, 1)].rearrange("b p t d -> (b p) t d"), y_out[:]).then_inc(s_out, 16)
                pool.wait_ge(s_out, 16 * i + 16)
                pool.sem_inc(s_alone, 1)

            def batch(i, ahead, start, more=False):
                if start:
                    split_normed_low(i + LEAD)
                pool.wait_ge(s_resid, x1_ready(i))
                keep_residual(i)
                if ahead:
                    residual(pool, i + 1)
                if start:
                    keep_tokens(i + LEAD)
                    decay_exponents(i + LEAD)
                    weigh_keys(i + LEAD)
                if more:
                    split_keys_low(i + LEAD + 1)
                store(i, i)

            pool.memset(ones[:], 1.0).then_inc(s_ident, 1)

            def load_weights(loads):
                for n in loads:
                    layer, units = LOADS[n]
                    start = sum(u for _, u in LOADS[:n]) * UNIT
                    part = slice(start, start + units * UNIT)
                    pool.dma_start(wgt[:, part], w_cols[:, part]).then_inc(s_wgt[layer], 16)

            load_weights((0, 1))
            keep_tokens(0)
            load_weights((2,))
            pool.wait_ge(s_mall, 16)
            mask_decay(0)
            load_weights((3, 4))
            weigh_keys(0)
            load_weights((5,))
            decay_exponents(1)
            load_weights((6,))
            weigh_keys(1)
            load_weights((7,))
            keep_tokens(1)
            load_weights((8,))
            split_keys_low(LEAD)
            with pool.Fori(0, BATCH - LEAD - 1) as i:
                batch(i, True, True, True)
            batch(BATCH - LEAD - 1, True, True)
            batch(BATCH - 2, True, False)
            batch(BATCH - 1, False, False)

            def general_path(i):
                pool.wait_ge(s_x1in, 16 * i + 16)
                keep_residual(BATCH + i)
                store(BATCH + i, i)

            if_general(pool, general_path)

        @block.scalar
        def _(act):
            def take_zT(j):
                act.wait_ge(s_zT, j + 1)
                act.activation(normed(j).rearrange("p c t -> p (c t)"), bank(j, 0), ACT.Copy).then_inc(s_zTe, 1)

            def split_normed(j):
                act.activation(normed_hi.rearrange("p c t -> p (c t)"), ps_a[0][:], ACT.Copy).then_inc(s_zhi, 1)

            def split_keys(j):
                act.wait_ge(*landed(j, s_ctxT, s_ctxT_early))
                act.activation(keys_hi, ctxT[:], ACT.Copy).then_inc(s_keys_hi, 1)

            def take_gate_low(j):
                act.wait_ge(s_gate, j + 1)
                act.activation(gate_low[:], ps_a[1][ROW_LOW:SPLIT_COLS, 0:SEQ], ACT.Copy).then_inc(s_gate_low, 1)

            def soft_cap(j):
                if plain(j):
                    act.wait_ge(s_gate, j + 1)
                    sums = bank(j, 1)
                else:
                    act.wait_ge(s_gate_sum, j - LEAD + 1)
                    sums = gate_sum[:]
                act.activation(rows[0:GATE_COLS], sums[0:GATE_COLS, 0:SEQ], ACT.Tanh, bias=gb[:], scale=1.0 / CAP).then_inc(s_gact, 1)

            def softplus(j):
                act.preload_act_table_set("natural_log_exp_and_others")
                act.wait_ge(s_gact, GATE_STEPS * j + 1)
                act.activation(f_row[:], rows[ROW_FLOOR:ROW_FLOOR + HEADS], ACT.Exp, scale=-CAP).then_inc(s_gact, 1)
                act.wait_ge(s_gact, GATE_STEPS * j + 2)
                act.activation(f_row[:], f_row[:], ACT.Ln, bias=1.0).then_inc(s_gact, 1)

            def take_cols(j):
                act.wait_ge(s_colT, j + 1)
                act.activation(cols[:].rearrange("p t r -> p (t r)"), bank(j, 1)[:, 0:TILES * ROWS], ACT.Copy).then_inc(s_cols, 1)

            def decay(j):
                act.wait_ge(s_cols, j + 1)
                reuse(act, s_num, j)
                for k, r0 in enumerate((ROW_FLOOR, ROW_CHUNK)):
                    last = act.activation(e_cols[:, :, k, :], cols[:, :, r0:r0 + HEADS], ACT.Exp)
                last.then_inc(s_ecols, 1)
                act.wait_ge(s_mask, TILES * (j + 1))
                reuse(act, s_pv, TILES * j)
                for r in range(ROWGRP):
                    d = maxima(j)[:, r:HEADS:ROWGRP, :].rearrange("p c (t q) -> p t c q", q=P)
                    act.activation(smat[:, r], d, ACT.Exp, scale=-1.0).then_inc(s_exp, 1)

            def take_near(j):
                act.wait_ge(s_pv, TILES * j + 1)
                act.activation(num[:, 0].rearrange("p h d -> p (h d)"), bank(j, 0)[:, 0:HEADS * DV], ACT.Copy).then_inc(s_near, 1)

            def take_z2T(j):
                act.wait_ge(s_z2T, j + 1)
                act.activation(z2_hi[:].rearrange("p c t -> p (c t)"), ps_a[0][:], ACT.Copy).then_inc(s_z2hi, 1)

            def silu(i, m):
                act.wait_ge(s_ab, KH * i + m + 1)
                act.activation(silu_a[:, m % 2], ps_f[m % 4][:, 0], ACT.Silu, scale=scl[:, 0, m:m + 1]).then_inc(s_silu, 1)

            def hi_1(i, m):
                act.wait_ge(s_hf, KH * i + m + 1)
                act.activation(h_hi[0][:, m], h_f[:, m % 2], ACT.Copy).then_inc(s_hi1, 1)

            def gelu(i, layer, m):
                n = 2 * KH * i + KH * layer + m
                act.wait_ge(s_mm, n + 1)
                if not (layer == 0 and m < GELU):
                    act.wait_ge(s_lo, n - GELU + 1)
                act.activation(gelu_f[:, m % GELU], ps_f[m % 4][:, 0], ACT.Gelu,
                               scale=scl[:, 2 + layer, m:m + 1]).then_inc(s_gelu, 1)
                act.wait_ge(s_gelu, n + 1)
                act.activation(h_hi[1 - layer][:, m], gelu_f[:, m % GELU], ACT.Copy).then_inc(s_hi, 1)

            def batch(i, ahead, start, more=False):
                j = i + LEAD
                for m in range(KH):
                    silu(i, m)
                    if m >= 1:
                        hi_1(i, m - 1)
                    if start and m == 3:
                        take_zT(j)
                        split_normed(j)
                hi_1(i, KH - 1)
                if start:
                    take_gate_low(j)
                    soft_cap(j)
                    softplus(j)
                for m in range(KH):
                    gelu(i, 0, m)
                    if start and m == 7:
                        take_cols(j)
                for m in range(KH):
                    gelu(i, 1, m)
                    if ahead and m == 0:
                        take_z2T(i + 1)
                    if start and m == 2:
                        decay(j)
                if start:
                    take_near(j)
                if more:
                    split_keys(j + 1)

            act.preload_act_table_set("exp_and_others")
            act.wait_ge(s_ready, 1)
            take_zT(0)
            soft_cap(0)
            softplus(0)
            take_cols(0)
            take_zT(1)
            soft_cap(1)
            softplus(1)
            decay(0)
            take_cols(1)
            take_near(0)
            decay(1)
            take_near(1)
            take_z2T(0)
            act.wait_ge(s_layer_const, 32)
            split_keys(LEAD)
            with act.Fori(0, BATCH - LEAD - 1) as i:
                batch(i, True, True, True)
            batch(BATCH - LEAD - 1, True, True)
            batch(BATCH - 2, True, False)
            batch(BATCH - 1, False, False)

            def general_path(i):
                take_z2T(BATCH + i)
                batch(BATCH + i, False, False)

            if_general(act, general_path)

        @block.vector
        def _(dve):
            count = {}

            def link(chain, base, ins):
                count[chain] = count.get(chain, 0) + 1
                ins.then_inc(chain, 1)
                dve.wait_ge(chain, base + count[chain])

            def rsqrt(chain, base, work, n):
                v, half, prod, y = (work[:, k, 0:n] for k in range(4))
                link(chain, base, dve.tensor_scalar(half.bitcast(I32), v.bitcast(I32), 1, None, ALU.logical_shift_right))
                link(chain, base, dve.tensor_scalar(y.bitcast(I32), half.bitcast(I32), -1.0, float(RSQRT_SEED), ALU.mult, ALU.add))
                for _ in range(3):
                    link(chain, base, dve.tensor_tensor(prod, y, y, ALU.mult))
                    link(chain, base, dve.scalar_tensor_tensor(prod, prod, -0.5, v, ALU.mult, ALU.mult))
                    link(chain, base, dve.scalar_tensor_tensor(y, prod, 1.5, y, ALU.add, ALU.mult))

            def norm_stats(chain, j, src):
                base = NORM_STEPS * j
                count[chain] = 0
                for t in range(TILES):
                    link(chain, base, dve.bn_stats(stats[:, t], src[:, t]))
                dve.sem_inc(s_alone, 1)
                for t in range(TILES):
                    last = dve.bn_aggr(mv[:, t], stats[:, t])
                link(chain, base, last)
                link(chain, base, dve.tensor_scalar(nw[:, 0, 0:TILES], mv[:, :, 1], LN_EPS, None, ALU.add))

            def norm_rsqrt(chain, j):
                rsqrt(chain, NORM_STEPS * j, nw, TILES)
                assert count[chain] == NORM_STEPS

            def norm_apply(j, src, dst, done):
                for t in range(TILES):
                    last = dve.tensor_scalar(dst[:, t], src[:, t], mv[:, t, 0:1], nw[:, 3, t:t + 1], ALU.subtract, ALU.mult)
                last.then_inc(done, 1)
                dve.wait_ge(done, j + 1)

            def norm_1_stats(j):
                dve.wait_ge(*landed(j, s_xin, s_xin_early))
                norm_stats(s_norm1, j, tokens(j))

            def norm_1_apply(j):
                reuse(dve, s_zT, j)
                norm_apply(j, tokens(j), z, s_z)

            def norm_2_stats(j):
                dve.wait_ge(s_resid, x1_ready(j))
                norm_stats(s_norm2, j, x1)

            def norm_2_apply(j):
                reuse(dve, s_z2T, j)
                norm_apply(j, x1, z2, s_z2)

            def norm_1(j):
                norm_1_stats(j)
                norm_rsqrt(s_norm1, j)
                norm_1_apply(j)

            def norm_2(j):
                norm_2_stats(j)
                norm_rsqrt(s_norm2, j)
                norm_2_apply(j)

            def split_gate_weights():
                dve.tensor_copy(gw_split[:, :, 0:GATE_COLS], gw[:]).then_inc(s_gw_split, 1)
                dve.tensor_copy(gw_split[:, :, GATE_COLS:ROW_LOW], gw[:, :, HEADS:HEADS + ROW_LOW - GATE_COLS]).then_inc(s_gw_split, 1)
                dve.wait_ge(s_gw_split, 2)
                dve.tensor_tensor(gw_split[:, :, ROW_LOW:SPLIT_COLS], gw[:], gw_split[:, :, 0:GATE_COLS].bitcast(F32), ALU.subtract)\
                   .then_inc(s_gw_split, 1)

            def add_gate_low(j):
                dve.wait_ge(s_gate_low, j - LEAD + 1)
                dve.tensor_tensor(gate_sum[:], ps_a[1][0:GATE_COLS, 0:SEQ], gate_low[:], ALU.add).then_inc(s_gate_sum, 1)

            def scans(j):
                dve.wait_ge(s_gact, GATE_STEPS * j + GATE_STEPS)
                n = SCAN_STEPS * j
                dve.tensor_tensor_scan(f_row[:], f_row[:], f_row[:], 0.0, ALU.add, ALU.max).then_inc(s_scan, 1)
                dve.wait_ge(s_scan, n + 1)
                g = rows[ROW_G:ROW_G + HEADS]
                dve.scalar_tensor_tensor(g, g, CAP, f_row[:], ALU.mult, ALU.add).then_inc(s_scan, 1)
                dve.wait_ge(s_scan, n + 2)
                reuse(dve, s_mst, 16 * j)
                dve.tensor_tensor_scan(m_row[:], g, g, -MASKED, ALU.max, ALU.max).then_inc(s_scan, 1)
                dve.wait_ge(s_scan, n + 3)
                c = m_row[:, P - 1:P]
                dve.tensor_tensor(rows[ROW_FLOOR:ROW_FLOOR + HEADS], f_row[:], m_row[:], ALU.subtract).then_inc(s_scan, 1)
                dve.tensor_scalar(rows[ROW_CHUNK:ROW_CHUNK + HEADS, 0:P], g[:, 0:P], c, None, ALU.subtract).then_inc(s_scan, 1)
                dve.tensor_scalar(rows[ROW_CHUNK:ROW_CHUNK + HEADS, P:SEQ], m_row[:, P:SEQ], -1.0, c, ALU.mult, ALU.add)\
                   .then_inc(s_scan, 1)

            def decay_shift(j):
                dve.wait_ge(s_mall, 16 * j + 16)
                dve.wait_ge(s_cols, j + 1)
                for t in range(TILES):
                    shift(dve, j, t).then_inc(s_decay_early, 1)

            def weigh_scores(j, groups):
                if 0 in groups:
                    dve.wait_ge(s_ecols, j + 1)
                    dve.tensor_scalar(floor[:], e_cols[:, :, 0, :], BACKEND_EPS, None, ALU.add).then_inc(s_floor, 1)
                for r in groups:
                    dve.wait_ge(s_qk, 2 * j + r // (ROWGRP // 2) + 1)
                    dve.wait_ge(s_exp, ROWGRP * j + r + 1)
                    s = smat[:, r].rearrange("p t c q -> p (t c q)")
                    dve.scalar_tensor_tensor(s, bank(j, r), SCORE_SCALE, s, ALU.mult, ALU.mult).then_inc(s_smat, 1)

            def take_state(j):
                dve.wait_ge(s_st, j + 1)
                dve.tensor_tensor(state[:], bank(j, 2)[:, 0:CH * ROWGRP * DV],
                                  head_mask[:].rearrange("p c h d -> p (c h d)"), ALU.mult).then_inc(s_state, 1)

            def take_far(j):
                dve.wait_ge(s_farmm, j + 1)
                u = e_cols[:, 1, 1, :].rearrange("p (h o) -> p h o", o=1).to_broadcast([P, HEADS, DV])
                dve.tensor_tensor(far[:], bank(j, 3)[:, 0:HEADS * DV].rearrange("p (h d) -> p h d", d=DV), u, ALU.mult)\
                   .then_inc(s_far, 1)
                dve.wait_ge(s_far, j + 1)
                dve.tensor_tensor(num[:, 1], bank(j, 1)[:, 0:HEADS * DV].rearrange("p (h d) -> p h d", d=DV), far[:], ALU.add)\
                   .then_inc(s_num, 1)

            def mix_divide(j):
                count[s_mix] = 0
                base = MIX_STEPS * j
                n = num[:].rearrange("p t h d -> p (t h) d")
                total = n[:, :, DH]
                dve.wait_ge(s_near, j + 1)
                dve.wait_ge(s_num, j + 1)
                dve.wait_ge(s_floor, j + 1)
                link(s_mix, base, dve.scalar_tensor_tensor(den[:, 0], total, -1.0, total, ALU.mult, ALU.max))
                link(s_mix, base, dve.scalar_tensor_tensor(den[:, 0], den[:, 0], BACKEND_EPS,
                                                           floor[:].rearrange("p t h -> p (t h)"), ALU.add, ALU.max))
                link(s_mix, base, dve.reciprocal(den[:, 1], den[:, 0]))
                per_head = den[:, 1].rearrange("p (h o) -> p h o", o=1).to_broadcast([P, TILES * HEADS, DH])
                link(s_mix, base, dve.tensor_tensor(h_att[:], n[:, :, 0:DH], per_head, ALU.mult))

            def mix_square(j):
                base = MIX_STEPS * j
                link(s_mix, base, dve.tensor_tensor(h_sq[:], h_att[:], h_att[:], ALU.mult))
                link(s_mix, base, dve.tensor_reduce(rms[:, 2], h_sq[:], AX.X, ALU.add))
                link(s_mix, base, dve.tensor_scalar(rms[:, 0], rms[:, 2], 1.0 / DH, RMS_EPS, ALU.mult, ALU.add))

            def mix_rsqrt(j):
                rsqrt(s_mix, MIX_STEPS * j, rms, TILES * HEADS)
                assert count[s_mix] == MIX_STEPS

            def take_z2T(j):
                dve.wait_ge(s_z2hi, j + 1)
                dve.tensor_tensor(z2_lo[:].rearrange("p c t -> p (c t)"), ps_a[0][:],
                                  z2_hi[:].rearrange("p c t -> p (c t)").bitcast(F32), ALU.subtract).then_inc(s_z2lo, 1)

            def swiglu(i, m):
                n = KH * i + m
                dve.wait_ge(s_silu, n + 1)
                if m >= 2:
                    dve.wait_ge(s_lo1, n - 1)
                dve.scalar_tensor_tensor(h_f[:, m % 2], ps_f[m % 4][:, 1], scl[:, 1, m:m + 1], silu_a[:, m % 2],
                                         ALU.mult, ALU.mult).then_inc(s_hf, 1)

            def lo_1(i, m):
                dve.wait_ge(s_hi1, KH * i + m + 1)
                dve.tensor_tensor(h_lo[0][:, m], h_f[:, m % 2], h_hi[0][:, m].bitcast(F32), ALU.subtract).then_inc(s_lo1, 1)

            def lo(i, layer, m):
                dve.wait_ge(s_hi, 2 * KH * i + KH * layer + m + 1)
                dve.tensor_tensor(h_lo[1 - layer][:, m], gelu_f[:, m % GELU], h_hi[1 - layer][:, m].bitcast(F32),
                                  ALU.subtract).then_inc(s_lo, 1)

            def finish(i):
                dve.wait_ge(s_x1f, i + 1)
                for t in range(TILES):
                    dve.wait_ge(s_ymm, TILES * i + t + 1)
                    dve.tensor_tensor(y_out[:, t], ps_f[LAST_BANKS[t]][:, 0], w3s_b[:], ALU.mult).then_inc(s_ysc, 1)
                for t in range(TILES):
                    dve.wait_ge(s_ysc, TILES * (i + 1) + t + 1)
                    dve.tensor_tensor(y_out[:, t], y_out[:, t], x1_ffn[:, t], ALU.add).then_inc(s_y, 1)

            def compare(i):
                for layer in range(LAYERS):
                    weights_in(dve, layer)
                dve.wait_ge(s_raw, 16 * i + 16)
                dve.sem_inc(s_alone, 1)
                dve.scalar_tensor_tensor(marks, raw, 1.0, wgt[:, bass.ds(i * COMPARE, COMPARE)].bitcast(F32),
                                         ALU.mult, ALU.not_equal, accum_out=inexact[:, bass.ds(i, 1)]).then_inc(s_inexact, 1)
                dve.wait_ge(s_inexact, i + 1)

            def decide():
                dve.tensor_reduce(inexact_sum[:], inexact[:], AX.X, ALU.add).then_inc(s_inexact_sum, 1)
                dve.wait_ge(s_inexact_all, 1)
                dve.tensor_scalar(general[:], ps_a[0][0:1, 0:1], 0.0, None, ALU.is_gt).then_inc(s_general, 1)

            def batch(i, ahead, start, more, check=True, last=False):
                j = i + LEAD
                for m in range(KH):
                    swiglu(i, m)
                    if m >= 1:
                        lo_1(i, m - 1)
                lo_1(i, KH - 1)
                if start:
                    add_gate_low(j)
                if ahead:
                    mix_divide(i + 1)
                    mix_square(i + 1)
                    mix_rsqrt(i + 1)
                if start:
                    scans(j)
                for m in range(KH):
                    lo(i, 0, m)
                    if ahead and m == 4:
                        norm_2_stats(i + 1)
                    if ahead and m == 6:
                        norm_rsqrt(s_norm2, i + 1)
                    if ahead and m == 7:
                        norm_2_apply(i + 1)
                for m in range(KH):
                    lo(i, 1, m)
                    if ahead and m == 0:
                        take_z2T(i + 1)
                    if check and m == 0:
                        compare(i)
                    if last and m == 1:
                        decide()
                    if more and m == 2:
                        norm_1_stats(j + 1)
                    if start and m in (3, 4):
                        weigh_scores(j, half_groups(m - 3))
                    if more and m == 5:
                        norm_rsqrt(s_norm1, j + 1)
                    if more and m == 6:
                        norm_1_apply(j + 1)
                if start:
                    take_state(j)
                finish(i)
                if start:
                    take_far(j)

            dve.sem_inc(s_ysc, TILES)
            dve.memset(rows[:], 0.0).then_inc(s_cleared, 1)
            dve.memset(gw[:], 0.0).then_inc(s_cleared, 1)
            dve.wait_ge(s_cleared, 2)
            dve.wait_ge(s_ident, 6)
            norm_1_stats(0)
            norm_rsqrt(s_norm1, 0)
            norm_1_apply(0)
            dve.wait_ge(s_const, 16 * 4)
            for k, r0 in enumerate((ROW_G, ROW_FLOOR)):
                w = gw_in[:, :, k * HEADS:(k + 1) * HEADS]
                dve.tensor_copy(gw[:, 0:CH, r0:r0 + HEADS], w[:, 0:CH])
                dve.tensor_tensor(gw[:, CH:2 * CH, r0:r0 + HEADS], w[:, CH:2 * CH], w[:, 2 * CH:3 * CH], ALU.add)
            dve.tensor_scalar(gb[:], gb_in[:], 1.0 / CAP, None, ALU.mult)
            dve.tensor_scalar(gain_b[:], gain_b[:], 1.0, None, ALU.add).then_inc(s_ready, 1)
            dve.wait_ge(s_ready, 1)
            norm_1(1)
            scans(0)
            norm_1(2)
            split_gate_weights()
            decay_shift(0)
            scans(1)
            weigh_scores(0, range(ROWGRP))
            take_state(0)
            take_far(0)
            mix_divide(0)
            mix_square(0)
            mix_rsqrt(0)
            residual(dve, 0)
            weigh_scores(1, range(ROWGRP))
            take_state(1)
            norm_2(0)
            take_far(1)
            take_z2T(0)
            dve.wait_ge(s_layer_const, 32)
            with dve.Fori(0, BATCH - LEAD - 1) as i:
                batch(i, True, True, True)
            batch(BATCH - LEAD - 1, True, True, False)
            batch(BATCH - 2, True, False, False)
            batch(BATCH - 1, False, False, False, last=True)

            def general_path(i):
                g = BATCH + i
                dve.wait_ge(s_x1in, 16 * i + 16)
                norm_stats(s_norm2, g, x1)
                norm_rsqrt(s_norm2, g)
                norm_2_apply(g)
                take_z2T(g)
                batch(g, False, False, False, check=False)

            if_general(dve, general_path)

        @block.tensor
        def _(pe):
            def turn(src, to, done):
                for c in range(CH):
                    for t in range(TILES):
                        col = c * SEQ + t * P
                        last = pe.transpose(to[:, col:col + P], src[:, t, c * P:(c + 1) * P], ident[:])
                last.then_inc(done, 1)

            def turn_z(j):
                pe.wait_ge(s_z, j + 1)
                if not early(j):
                    reuse(pe, s_near, j)
                turn(z, bank(j, 0), s_zT)

            def turn_z2(j):
                pe.wait_ge(s_z2, j + 1)
                turn(z2, ps_a[0][:], s_z2T)

            def split_gates(j):
                pe.wait_ge(s_gw_split, 3)
                pe.wait_ge(s_keys_lo, j - LEAD + 1)
                for c in range(CH):
                    for part in (keys_hi, keys_lo):
                        pe.matmul(ps_a[1][0:SPLIT_COLS, 0:SEQ], gw_split[:, CH + c], part[:, c], start=(c == 0 and part is keys_hi),
                                  stop=False)
                pe.wait_ge(s_zlo, j - LEAD + 1)
                for c in range(CH):
                    for part in (normed_hi, normed_lo):
                        last = pe.matmul(ps_a[1][0:SPLIT_COLS, 0:SEQ], gw_split[:, c], part[:, c], start=False,
                                         stop=(c == CH - 1 and part is normed_lo))
                last.then_inc(s_gate, 1)

            def gates(j):
                pe.wait_ge(s_zTe, j + 1)
                pe.wait_ge(*landed(j, s_ctxT, s_ctxT_early))
                if not early(j):
                    reuse(pe, s_num, j)
                if not plain(j):
                    split_gates(j)
                    return
                for c in range(CH):
                    pe.matmul(bank(j, 1)[0:GATE_COLS, 0:SEQ], gw[:, CH + c], keys(j)[:, c], start=(c == 0), stop=False)
                for c in range(CH):
                    last = pe.matmul(bank(j, 1)[0:GATE_COLS, 0:SEQ], gw[:, c], normed(j)[:, c], start=False, stop=(c == CH - 1))
                last.then_inc(s_gate, 1)

            def turn_rows(j):
                pe.wait_ge(s_scan, SCAN_STEPS * j + SCAN_STEPS)
                for t in range(TILES):
                    last = pe.transpose(bank(j, 1)[:, t * ROWS:(t + 1) * ROWS], rows[:, t * P:(t + 1) * P], ident[0:ROWS, 0:ROWS])
                last.then_inc(s_colT, 1)

            def scores(j, groups):
                if 0 in groups:
                    pe.wait_ge(s_cols, j + 1)
                    if not early(j):
                        reuse(pe, s_z2lo, j)
                for t in range(TILES):
                    for c in range(CH):
                        for r in groups:
                            d = slice(r * DH, (r + 1) * DH)
                            col = (t * CH + c) * P
                            last = pe.matmul(bank(j, r)[:, col:col + P], keys(j)[d, c, t * P:(t + 1) * P],
                                             normed(j)[d, c, t * P:(t + 1) * P], start=True, stop=True)
                last.then_inc(s_qk, 1)

            def make_state(j):
                pe.wait_ge(s_kwt, j + 1)
                pe.wait_ge(s_smat, ROWGRP * j + 3)
                for c in range(CH):
                    h = slice(c * ROWGRP, (c + 1) * ROWGRP)
                    last = pe.matmul(bank(j, 2)[:, c * ROWGRP * DV:(c + 1) * ROWGRP * DV], k_wt[:, h, :], v_aug[:, 0, h, :],
                                     start=True, stop=True)
                last.then_inc(s_st, 1)

            def values(j, tiles):
                pe.wait_ge(s_smat, ROWGRP * j + ROWGRP)
                pe.wait_ge(s_v, 16 * j + 16)
                for t in tiles:
                    for h in range(HEADS):
                        last = pe.matmul(bank(j, t)[:, h * DV:(h + 1) * DV], smat[:, h % ROWGRP, t, h // ROWGRP, :],
                                         v_aug[:, t, h, :], start=True, stop=True)
                    last.then_inc(s_pv, 1)

            def read_state(j):
                pe.wait_ge(s_state, j + 1)
                for c in range(CH):
                    part = slice(c * ROWGRP * DV, (c + 1) * ROWGRP * DV)
                    last = pe.matmul(bank(j, 3)[:, part], normed(j)[:, c, P:SEQ], state[:, part], start=True, stop=True)
                last.then_inc(s_farmm, 1)

            def columns(u, col, width, as_is):
                if as_is:
                    slot = ORDER.index(u) % STAGE
                    return stage[:, slot * UNIT + col:slot * UNIT + col + width]
                return wgt[:, u * UNIT + col:u * UNIT + col + width]

            def moving(a, as_is):
                return a.bitcast(F32) if as_is else a

            def swiglu(i, m, as_is):
                if m in LAST_BANKS:
                    pe.wait_ge(s_ysc, TILES * i + LAST_BANKS.index(m) + 1)
                if m >= 4:
                    pe.wait_ge(s_hf, KH * i + m - 3)
                per = KH // N_W1
                for half, base in enumerate((UNIT_W1, UNIT_W2)):
                    if as_is and m % per == 0:
                        pe.wait_ge(*unit_landed(i - BATCH, base + m // per))
                    for c in range(CH):
                        w = columns(base + m // per, (m % per * CH + c) * P, P, as_is)
                        pe.matmul(ps_f[m % 4][:, half], w, moving(z2_hi[:, c], as_is), start=(c == 0), stop=False)
                        last = pe.matmul(ps_f[m % 4][:, half], w, moving(z2_lo[:, c], as_is), start=False, stop=(c == CH - 1))
                last.then_inc(s_ab, 1)

            def hidden(i, layer, m, ks, as_is):
                group = KH * layer + m
                unit = UNIT_H1 + group
                if ks[0] == 0:
                    if as_is:
                        pe.wait_ge(*unit_landed(i - BATCH, unit))
                    if group < 4:
                        pe.wait_ge(s_hf, KH * i + m + 5)
                    else:
                        pe.wait_ge(s_gelu, 2 * KH * i + group - 3)
                for k in ks:
                    if m < 2:
                        if layer == 0:
                            pe.wait_ge(s_lo1, KH * i + k + 1)
                        else:
                            pe.wait_ge(s_lo, 2 * KH * i + k + 1)
                    w = columns(unit, k * P, P, as_is)
                    pe.matmul(ps_f[m % 4][:, 0], w, moving(h_hi[layer][:, k], as_is), start=(k == 0), stop=False)
                    last = pe.matmul(ps_f[m % 4][:, 0], w, moving(h_lo[layer][:, k], as_is), start=False, stop=(k == KH - 1))
                if ks[-1] == KH - 1:
                    last.then_inc(s_mm, 1)

            def hidden_layer(i, layer, as_is, after):
                for k in range(KH - 1):
                    for m in range(2):
                        hidden(i, layer, m, (k,), as_is)
                for m in range(2):
                    hidden(i, layer, m, range(KH - 1, KH), as_is)
                    after(m)
                for m in range(2, KH):
                    hidden(i, layer, m, range(KH), as_is)
                    after(m)

            def project(i, as_is):
                per = UNIT // DIM

                def part(t, ks):
                    for k in ks:
                        if as_is and k % per == 0:
                            pe.wait_ge(*unit_landed(i - BATCH, UNIT_W3 + k // per))
                        pe.wait_ge(s_lo, 2 * KH * i + KH + max(k + 1, LAST_BANKS[t] + 5))
                        w = columns(UNIT_W3 + k // per, k % per * DIM, DIM, as_is)
                        pe.matmul(ps_f[LAST_BANKS[t]][:, 0], moving(h_hi[0][:, k, t * P:(t + 1) * P], as_is), w, start=(k == 0), stop=False)
                        last = pe.matmul(ps_f[LAST_BANKS[t]][:, 0], moving(h_lo[0][:, k, t * P:(t + 1) * P], as_is), w, start=False,
                                         stop=(k == KH - 1))
                    return last

                for t in range(TILES):
                    part(t, range(KH - 1))
                for t in range(TILES):
                    part(t, range(KH - 1, KH)).then_inc(s_ymm, 1)

            def count_inexact():
                pe.wait_ge(s_inexact_sum, 1)
                pe.matmul(ps_a[0][0:1, 0:1], inexact_sum[:], ones[:], start=True, stop=True).then_inc(s_inexact_all, 1)

            def batch(i, ahead, start, as_is=False, last=False):
                j = i + LEAD
                weights_in(pe, 0)
                pe.wait_ge(s_z2lo, i + 1)
                for m in range(KH):
                    swiglu(i, m, as_is)
                    if start and m == 1:
                        turn_z(j)
                if start:
                    gates(j)

                def after_2(m):
                    if start and m == 6:
                        turn_rows(j)

                def after_3(m):
                    if ahead and m == 1:
                        turn_z2(i + 1)
                    if start and m in (2, 3):
                        scores(j, half_groups(m - 2))
                    if last and m == 3:
                        count_inexact()
                    if start and m == 7:
                        make_state(j)
                        values(j, (0,))

                weights_in(pe, 1)
                hidden_layer(i, 0, as_is, after_2)
                weights_in(pe, 2)
                hidden_layer(i, 1, as_is, after_3)
                weights_in(pe, 3)
                project(i, as_is)
                if start:
                    values(j, (1,))
                    read_state(j)

            def keep_clock(to, products):
                for _ in range(products):
                    pe.matmul(to[:, 0:P], ident[:], ident[:], start=True, stop=True)

            def attend(j):
                make_state(j)
                values(j, range(TILES))
                read_state(j)

            pe.wait_ge(s_ident, 6)
            pe.wait_ge(s_cleared, 2)
            keep_clock(bank(0, 3), 12)
            turn_z(0)
            pe.wait_ge(s_ready, 1)
            gates(0)
            keep_clock(bank(0, 3), 12)
            turn_z(1)
            keep_clock(bank(0, 3), 8)
            turn_rows(0)
            keep_clock(bank(0, 3), 4)
            gates(1)
            for half in range(2):
                scores(0, half_groups(half))
            keep_clock(bank(1, 3), 24)
            attend(0)
            turn_rows(1)
            for half in range(2):
                scores(1, half_groups(half))
            pe.wait_ge(s_num, 1)
            keep_clock(bank(0, 3), 12)
            attend(1)
            keep_clock(bank(0, 3), 1)
            turn_z2(0)
            keep_clock(bank(0, 3), 3)
            with pe.Fori(0, BATCH - LEAD) as i:
                batch(i, True, True)
            batch(BATCH - 2, True, False)
            batch(BATCH - 1, False, False, last=True)

            def general_path(i):
                turn_z2(BATCH + i)
                batch(BATCH + i, False, False, as_is=True)

            if_general(pe, general_path)


def kernel(x, ctx_1024, L0_xattn_ifgate_w, L0_xattn_ifgate_b, L0_xattn_outnorm_w, L0_ffn_w1_w, L0_ffn_w1_s, L0_ffn_w2_w,
           L0_ffn_w2_s, L0_ffn_h1_w, L0_ffn_h1_s, L0_ffn_h2_w, L0_ffn_h2_s, L0_ffn_w3_w, L0_ffn_w3_s):
    import concourse.bacc as bacc
    from concourse.bass_utils import run_bass_kernel_spmd

    def tok(a):
        return np.ascontiguousarray(np.asarray(a).reshape(BATCH, TILES, P, DIM).transpose(0, 2, 1, 3))

    ctx = np.asarray(ctx_1024)
    v_aug = np.ones((BATCH, P, TILES, HEADS, DV), np.float32)
    v_aug[..., 0:DH] = tok(ctx).reshape(BATCH, P, TILES, HEADS, DH)
    ctx_t = np.ascontiguousarray(ctx.reshape(BATCH, SEQ, CH, P).transpose(0, 3, 2, 1))

    def up(w):
        return np.asarray(w).reshape(N_W1, KH // N_W1, P, CH, P).transpose(0, 4, 1, 3, 2).reshape(N_W1, P, UNIT)

    def square(w):
        return np.asarray(w).reshape(KH, P, KH, P).transpose(0, 3, 2, 1).reshape(KH, P, UNIT)

    def down(w):
        n = KH * DIM // UNIT
        return np.asarray(w).reshape(DIM, n, KH // n, P).transpose(1, 3, 2, 0).reshape(n, P, UNIT)

    w_units = np.concatenate([up(L0_ffn_w1_w), up(L0_ffn_w2_w), square(L0_ffn_h1_w), square(L0_ffn_h2_w),
                              down(L0_ffn_w3_w)])
    w_cols = np.ascontiguousarray(w_units.transpose(1, 0, 2).reshape(P, COLS))
    scales = np.ascontiguousarray(np.stack([np.asarray(s).reshape(KH, P) for s in
                                            (L0_ffn_w1_s, L0_ffn_w2_s, L0_ffn_h1_s, L0_ffn_h2_s)]).transpose(2, 0, 1))
    gate_w = np.ascontiguousarray(np.asarray(L0_xattn_ifgate_w).reshape(2 * HEADS, 3 * CH, P).transpose(2, 1, 0))
    arrays = {
        "x": tok(x), "ctx_tok": v_aug, "ctx_t": ctx_t, "gate_w": gate_w,
        "gate_b": np.ascontiguousarray(np.asarray(L0_xattn_ifgate_b).reshape(2, HEADS, 1)),
        "outnorm_w": np.ascontiguousarray(np.asarray(L0_xattn_outnorm_w).reshape(1, DIM)),
        "w_cols": w_cols, "scales": scales, "w3_s": np.ascontiguousarray(np.asarray(L0_ffn_w3_s).reshape(1, DIM)),
    }
    nc = bacc.Bacc("TRN2", target_bir_lowering=False, num_devices=1)
    args = {n: nc.dram_tensor(n, a.shape, F32, kind="ExternalInput").ap() for n, a in arrays.items()}
    out = nc.dram_tensor("out", (BATCH, P, TILES, DIM), F32, kind="ExternalOutput").ap()
    build(nc, out=out, **args)
    got = run_bass_kernel_spmd(nc, [arrays], core_ids=[0]).results[0]["out"]
    return np.ascontiguousarray(np.asarray(got).transpose(0, 2, 1, 3).reshape(BATCH, SEQ, DIM))
```
